# Optimizing a Trainium2 kernel written in Bass

```python
import numpy as np
import jax
import jax.numpy as jnp

def _softmax(x, axis=-1):
    return jax.nn.softmax(x, axis=axis)

def _gelu(x):
    return jax.nn.gelu(x, approximate=True)

def _silu(x):
    return jax.nn.silu(x)

def _sigmoid(x):
    return jax.nn.sigmoid(x)

def _layernorm(x, axis=-1, eps=1e-05):
    m = jnp.mean(x, axis=axis, keepdims=True)
    v = jnp.var(x, axis=axis, keepdims=True)
    return (x - m) / jnp.sqrt(v + eps)

def _scatter_add(tgt, idx, src, axis=0):
    return tgt.at[idx].add(src)

def _segment_sum(src, seg, n):
    return jax.ops.segment_sum(src, seg, n)
kernel_name = 'mk_adj_resnorm_d2_adj_r2_3860de'

def setup_inputs(seed: int=0):
    np.random.seed(seed)
    _w = jnp.asarray

    def _rec_inputs():
        import jax
        import jax.numpy as jnp
        _gk = jax.random.key(seed)
        x = -0.000125 + 0.9999 * jax.random.normal(jax.random.fold_in(_gk, 1), (64, 128, 128), jnp.float32)
        _w = (1.0 + jnp.arange(128, dtype=jnp.float32)) ** (-0.5)
        _w = _w / _w.mean()
        _pij = jnp.clip(0.015625 * _w[:, None] * _w[None, :], 0.0, 1.0)
        _a = jax.random.uniform(jax.random.fold_in(_gk, 2), (128, 128)) < _pij
        _a = jnp.logical_or(_a, jnp.swapaxes(_a, -1, -2))
        _a = jnp.logical_or(_a, jnp.eye(128, dtype=bool))
        _af = _a.astype(jnp.float32)
        _af = _af * jax.random.uniform(jax.random.fold_in(_gk, 3), (128, 128), jnp.float32, 0.05, 0.000488281)
        adj = _af
        return (x, adj)
    x, adj = _rec_inputs()

    def _L0_gnn_setup():
        import jax, jax.numpy as jnp
        import numpy as np
        B, T, D, H = (64, 1024, 128, 128)
        MAX_SKIP = 4

        def _lstm_last(Wih, Whh, bih, bhh, xs):
            N, _, Hd = xs.shape
            bias = bih + bhh

            def step(carry, x_t):
                h, c = carry
                g = x_t @ Wih.T + h @ Whh.T + bias
                i, f, gg, o = jnp.split(g, 4, axis=-1)
                c = jax.nn.sigmoid(f) * c + jax.nn.sigmoid(i) * jnp.tanh(gg)
                h = jax.nn.sigmoid(o) * jnp.tanh(c)
                return ((h, c), None)
            init = (jnp.zeros((N, Hd), xs.dtype), jnp.zeros((N, Hd), xs.dtype))
            (h_last, _), _ = jax.lax.scan(step, init, jnp.swapaxes(xs, 0, 1))
            return h_last
        key = jax.random.key(seed)
        ks = jax.random.split(key, 8)
        s = 0.05
        x = jax.random.normal(ks[0], (B, T, D), jnp.float32)
        adj = jax.random.uniform(ks[1], (T, T), jnp.float32) / T
        Wg0 = jax.random.normal(ks[2], (D, H), jnp.float32) * s
        bg0 = jnp.zeros((H,), jnp.float32)
        Wg1 = jax.random.normal(ks[3], (H, H), jnp.float32) * s
        bg1 = jnp.zeros((H,), jnp.float32)
        Wih = jax.random.normal(ks[4], (MAX_SKIP, 4 * H, H), jnp.float32) * s
        Whh = jax.random.normal(ks[5], (MAX_SKIP, 4 * H, H), jnp.float32) * s
        bih = jax.random.normal(ks[6], (MAX_SKIP, 4 * H), jnp.float32) * s
        bhh = jax.random.normal(ks[7], (MAX_SKIP, 4 * H), jnp.float32) * s
        return dict(x=x, adj=adj, Wg0=Wg0, bg0=bg0, Wg1=Wg1, bg1=bg1, Wih=Wih, Whh=Whh, bih=bih, bhh=bhh)
    _L0_gnn_all = _L0_gnn_setup()
    _L0_gnn_in = {k: v for k, v in _L0_gnn_all.items() if k in ('Wg0', 'bg0', 'Wg1', 'bg1', 'Wih', 'Whh', 'bih', 'bhh')}
    del _L0_gnn_all

    def _L1_gnn_setup():
        import jax, jax.numpy as jnp
        import numpy as np
        B, N, IN_DIM, OUT_DIM, H = (2, 2048, 128, 128, 4)
        HEAD_DIM = OUT_DIM // H
        EDGE_P = 0.01
        key = jax.random.key(seed)
        k1, k2, k3 = jax.random.split(key, 3)
        h = jax.random.normal(k1, (B, N, IN_DIM), dtype=jnp.float32)
        W = jax.random.normal(k2, (IN_DIM, 3 * OUT_DIM), dtype=jnp.float32) / np.sqrt(IN_DIM)
        adj = (jax.random.uniform(k3, (N, N)) < EDGE_P).astype(jnp.float32)
        adj = jnp.maximum(adj, jnp.eye(N, dtype=jnp.float32))
        return {'h': h, 'W': W, 'adj': adj}
    _L1_gnn_all = _L1_gnn_setup()
    _L1_gnn_in = {k: v for k, v in _L1_gnn_all.items() if k in ('W',)}
    del _L1_gnn_all
    return {'x': x, 'adj': adj, 'L0_gnn_Wg0': _L0_gnn_in['Wg0'], 'L0_gnn_bg0': _L0_gnn_in['bg0'], 'L0_gnn_Wg1': _L0_gnn_in['Wg1'], 'L0_gnn_bg1': _L0_gnn_in['bg1'], 'L0_gnn_Wih': _L0_gnn_in['Wih'], 'L0_gnn_Whh': _L0_gnn_in['Whh'], 'L0_gnn_bih': _L0_gnn_in['bih'], 'L0_gnn_bhh': _L0_gnn_in['bhh'], 'L1_gnn_W': _L1_gnn_in['W']}

def reference(x, adj, L0_gnn_Wg0, L0_gnn_bg0, L0_gnn_Wg1, L0_gnn_bg1, L0_gnn_Wih, L0_gnn_Whh, L0_gnn_bih, L0_gnn_bhh, L1_gnn_W):
    import jax
    import jax.numpy as jnp

    def _L0_gnn_ref(x, adj, Wg0, bg0, Wg1, bg1, Wih, Whh, bih, bhh):
        import jax, jax.numpy as jnp
        import numpy as np
        B, T, D, H = (64, 1024, 128, 128)
        MAX_SKIP = 4

        def _lstm_last(Wih, Whh, bih, bhh, xs):
            N, _, Hd = xs.shape
            bias = bih + bhh

            def step(carry, x_t):
                h, c = carry
                g = x_t @ Wih.T + h @ Whh.T + bias
                i, f, gg, o = jnp.split(g, 4, axis=-1)
                c = jax.nn.sigmoid(f) * c + jax.nn.sigmoid(i) * jnp.tanh(gg)
                h = jax.nn.sigmoid(o) * jnp.tanh(c)
                return ((h, c), None)
            init = (jnp.zeros((N, Hd), xs.dtype), jnp.zeros((N, Hd), xs.dtype))
            (h_last, _), _ = jax.lax.scan(step, init, jnp.swapaxes(xs, 0, 1))
            return h_last
        h = jax.nn.relu(jnp.einsum('ts,bsh->bth', adj, x @ Wg0 + bg0))
        h = jax.nn.relu(jnp.einsum('ts,bsh->bth', adj, h @ Wg1 + bg1))
        Bv, Tv, Hd = h.shape
        for p in range(1, MAX_SKIP + 1):
            nw = Tv // p
            wins = h[:, :nw * p, :].reshape(Bv * nw, p, Hd)
            last = _lstm_last(Wih[p - 1], Whh[p - 1], bih[p - 1], bhh[p - 1], wins)
            idx = jnp.arange(nw) * p + (p - 1)
            h = h.at[:, idx, :].set(last.reshape(Bv, nw, Hd))
        return h

    def _L1_gnn_ref(h, W, adj):
        import jax, jax.numpy as jnp
        import numpy as np
        B, N, IN_DIM, OUT_DIM, H = (2, 2048, 128, 128, 4)
        HEAD_DIM = OUT_DIM // H
        EDGE_P = 0.01
        Bn, Nn, _ = h.shape
        qkv = h @ W
        qkv = qkv.reshape(Bn, Nn, 3, H, HEAD_DIM).transpose(2, 0, 3, 1, 4)
        q, k, v = (qkv[0], qkv[1], qkv[2])
        mask = jnp.where(adj == 0, -jnp.inf, 0.0)
        scores = jnp.einsum('bhid,bhjd->bhij', q, k) / np.sqrt(HEAD_DIM) + mask
        attn = jax.nn.softmax(scores, axis=-1)
        out = jnp.einsum('bhij,bhjd->bhid', attn, v)
        return out.transpose(0, 2, 1, 3).reshape(Bn, Nn, OUT_DIM)
    x = _layernorm(x + _L0_gnn_ref(x, adj, L0_gnn_Wg0, L0_gnn_bg0, L0_gnn_Wg1, L0_gnn_bg1, L0_gnn_Wih, L0_gnn_Whh, L0_gnn_bih, L0_gnn_bhh), axis=-1)
    x = _layernorm(x + _L1_gnn_ref(x, L1_gnn_W, adj), axis=-1)
    return x

_drawn_inputs = setup_inputs


def setup_inputs(seed=0):
    import zlib

    import numpy as np

    out = dict(_drawn_inputs(seed))
    spreads = {'L0_gnn_bg0': (0.0, 0.8), 'L0_gnn_bg1': (0.0, 0.8)}
    factors = {'L0_gnn_Wg0': 8.0, 'L0_gnn_Wg1': 8.0, 'L0_gnn_Wih': 8.0, 'L0_gnn_Whh': 8.0}
    for name, (base, spread) in spreads.items():
        noise = np.random.default_rng([zlib.crc32(name.encode()), seed]).standard_normal(out[name].shape)
        drawn = base * np.exp(spread * noise) if base else spread * noise
        out[name] = jnp.asarray(drawn.astype(out[name].dtype))
    for name, factor in factors.items():
        out[name] = (out[name] * factor).astype(out[name].dtype)
    return out
```

```python
from contextlib import ExitStack

import concourse.bass as bass
from concourse import mybir



class Turn:

    def __init__(self, number, register=None, stride=0):
        self.number, self.register, self.stride = number, register, stride

    def times(self, per, plus=0):
        fixed = self.number * per + plus
        return fixed if self.register is None else self.register * (self.stride * per) + fixed

    def parity(self):
        return self.number % 2


def turns(engine, first, loop_from, loop_to, last):
    for n in range(first, loop_from):
        yield Turn(n)
    with engine.Fori(0, (loop_to - loop_from + 1) // 2) as i:
        yield Turn(loop_from, i, 2)
        yield Turn(loop_from + 1, i, 2)
    for n in range(loop_to + 1, last + 1):
        yield Turn(n)


def gnn_lstm_attention(nc, x, adj, Wg0, bg0, Wg1, bg1, Wih, Whh, bih, bhh, Wqkv, out):
    F32, F32R = mybir.dt.float32, mybir.dt.float32r
    ALU, ACT, AX = mybir.AluOpType, mybir.ActivationFunctionType, mybir.AxisListType

    B, T, D = x.shape
    SKIPS = Wih.shape[0]
    HEADS, HD = 4, D // 4
    EPS = 1e-5
    MASKED = -3e38
    GB = 4
    GC = GB * T
    NG = B // GB
    BANK = 512
    GATE_I, GATE_F, GATE_G, GATE_O = range(4)
    FIRST_STEP = (GATE_I, GATE_G, GATE_O)
    LATER_STEP = (GATE_F, GATE_I, GATE_G, GATE_O)
    VW = 64

    TILE_GRAPHS = {1: 4, 2: 8, 3: 8, 4: 16}
    WINDOWS = {p: T // p for p in TILE_GRAPHS}
    COLS = {p: TILE_GRAPHS[p] * WINDOWS[p] for p in TILE_GRAPHS}
    PAIRS = {p: B // (2 * TILE_GRAPHS[p]) for p in TILE_GRAPHS}
    STEPS_BEFORE, FORGETS_BEFORE, total, forgets = {}, {}, 0, 0
    for p in TILE_GRAPHS:
        STEPS_BEFORE[p], FORGETS_BEFORE[p] = total, forgets
        total += PAIRS[p] * 2 * p
        forgets += PAIRS[p] * 2 * (p - 1)
    ALL_STEPS, ALL_FORGETS = total, forgets

    SPARE = 4

    def seen(n):
        return n + SPARE

    ctx = ExitStack()
    with ctx:
        def sb(name, shape, dt=F32):
            return ctx.enter_context(nc.sbuf_tensor(name, shape, dt))

        def sem(name):
            return ctx.enter_context(nc.semaphore(name))

        counters = []

        def counter(name):
            counters.append(sem(name))
            return counters[-1]

        bank = ctx.enter_context(nc.psum_tensor("bank", [128, 8, BANK], F32))

        seq_hi = sb("seq_hi", [D, B * T], F32R)
        seq_lo = sb("seq_lo", [D, B * T], F32R)
        wih_hi = sb("wih_hi", [D, SKIPS, 4 * D], F32R)
        wih_lo = sb("wih_lo", [D, SKIPS, 4 * D], F32R)
        whh_hi = sb("whh_hi", [D, SKIPS, 4 * D], F32R)
        whh_lo = sb("whh_lo", [D, SKIPS, 4 * D], F32R)
        state_hi = sb("state_hi", [D, 2, BANK], F32R)
        state_lo = sb("state_lo", [D, 2, BANK], F32R)

        ident = sb("ident", [128, 128])
        adj_nat = sb("adj_nat", [T, T])
        adj_t = sb("adj_t", [T, T])
        mask = sb("mask", [T, T])
        w0 = sb("w0", [D, D])
        w1 = sb("w1", [D, D])
        wqkv = sb("wqkv", [D, 3 * D])
        b0_rows = sb("b0_rows", [128, D])
        b1_rows = sb("b1_rows", [128, D])
        b0_term = sb("b0_term", [D, T])
        b_in = sb("b_in", [SKIPS * 4, 2, D])
        b_sum = sb("b_sum", [SKIPS * 4, D])
        gate_bias = sb("gate_bias", [D, SKIPS * 4])
        head_mask = sb("head_mask", [D, HEADS])
        minus_half = sb("minus_half", [128, GB])
        eps = sb("eps", [128, GB])

        early = sb("early", [128, 22 * BANK])
        late = sb("late", [128, 18 * BANK])

        def part(region, at, n):
            return region[:, at * BANK:(at + n) * BANK].rearrange("p (n c) -> p n c", c=BANK)

        x_tile = part(early, 0, 2)
        ax_sb = part(early, 2, 2)
        h0_pre = part(early, 4, 1)
        h0 = part(early, 5, 2)
        u_sb = part(early, 7, 2)
        h1 = part(early, 9, 2)
        w_nat = early[:, 11 * BANK:18 * BANK]
        w_half = part(early, 18, 2)
        gates = late[:, 0:8 * BANK].rearrange("p (s g c) -> p s g c", s=2, g=4)
        cell = part(late, 8, 2)
        kept = part(late, 10, 2)
        added = part(late, 12, 2)
        tanh_cell = part(late, 14, 2)
        state = part(late, 16, 2)
        x_res = part(early, 0, 2)
        h_sum = part(early, 2, 2)
        resid = part(early, 4, 2)
        x1 = part(early, 6, 2)
        x1_t = part(early, 8, 2)
        v_aug = early[:, 10 * BANK:14 * BANK].rearrange("p (r b h w) -> p r b h w", r=2, b=GB, h=HEADS)
        y = part(early, 14, 2)
        out_tile = part(early, 16, 2)
        attended = part(early, 18, 2)
        q_t = part(early, 20, 2)
        k_exp = late[:, 0:8 * BANK].rearrange("p (r h c) -> p r h c", r=2, h=HEADS)
        masked = part(late, 8, 2)
        prob = part(late, 10, 2)
        prob_t = part(late, 12, 2)
        k_t = part(late, 14, 1)
        stats = sb("stats", [128, GB, 6])
        moments = sb("moments", [128, 2, GB, 2])
        var_eps = sb("var_eps", [128, GB])
        rstd = sb("rstd", [128, 2, GB])
        shift = sb("shift", [128, 2, GB])
        neg_max = sb("neg_max", [128, 2, HEADS])
        rec = sb("rec", [128, 2, HEADS])

        weights_in = sem("weights_in")
        lstm_in = sem("lstm_in")
        consts_made = sem("consts_made")
        setup_mm = sem("setup_mm")
        setup_out = sem("setup_out")
        wt_made = sem("wt_made")
        wt_half = counter("wt_half")
        wt_hi = sem("wt_hi")
        wt_lo = counter("wt_lo")
        mask_step = sem("mask_step")
        x_in = [sem(f"x_in_{n}") for n in "01"]
        ax_made = counter("ax_made")
        ax_out = counter("ax_out")
        h0_made = counter("h0_made")
        h0_biased = counter("h0_biased")
        h0_out = counter("h0_out")
        u_made = counter("u_made")
        u_out = counter("u_out")
        h1_made = counter("h1_made")
        h1_out = counter("h1_out")
        h1_hi = counter("h1_hi")
        h1_lo = counter("h1_lo")
        gate_made = [counter(f"gate_made_{g}") for g in "ifgo"]
        gate_active = [counter(f"gate_active_{g}") for g in "ifgo"]
        term_made = counter("term_made")
        cell_made = counter("cell_made")
        tanh_made = counter("tanh_made")
        state_made = counter("state_made")
        state_hi_made = counter("state_hi_made")
        state_lo_made = counter("state_lo_made")
        ones_made = sem("ones_made")
        res_in = [sem(f"res_in_{n}") for n in "01"]
        hsum_made = counter("hsum_made")
        ht_made = counter("ht_made")
        resid_made = counter("resid_made")
        bn_made = [counter(f"bn_made_{norm}") for norm in "12"]
        mom_made = [counter(f"mom_made_{norm}") for norm in "12"]
        eps_made = [counter(f"eps_made_{norm}") for norm in "12"]
        rstd_made = [counter(f"rstd_made_{norm}") for norm in "12"]
        shift_made = [counter(f"shift_made_{norm}") for norm in "12"]
        x1_made = counter("x1_made")
        x1t_made = counter("x1t_made")
        x1t_out = counter("x1t_out")
        k_made = counter("k_made")
        k_out = counter("k_out")
        k_spread = counter("k_spread")
        q_made = counter("q_made")
        q_out = counter("q_out")
        v_made = counter("v_made")
        v_out = counter("v_out")
        scores_made = counter("scores_made")
        masked_made = counter("masked_made")
        max_made = counter("max_made")
        prob_made = counter("prob_made")
        probt_made = counter("probt_made")
        probt_out = counter("probt_out")
        pv_made = counter("pv_made")
        rec_made = counter("rec_made")
        attended_made = counter("attended_made")
        y_made = counter("y_made")
        out_made = counter("out_made")
        stored = [counter(f"stored_{n}") for n in "01"]

        def group_turns(engine, first, last):
            return turns(engine, first, 1, NG - 2, last)

        def exists(turn, back=0):
            return 0 <= turn.number - back < NG

        def seq_cols(seq, p, pair, stream, k):
            width = TILE_GRAPHS[p] * T
            tile = seq[:, bass.ds(pair.times(2 * width, stream * width), width)]
            if T % p == 0:
                return tile.rearrange("d (w p) -> d w p", p=p)[:, :, k]
            return tile.rearrange("d (b t) -> d b t", t=T)[:, :, k:k + p * (WINDOWS[p] - 1) + 1:p]

        def shaped(ap, p):
            ap = ap[:, 0:COLS[p]]
            return ap if T % p == 0 else ap.rearrange("d (b w) -> d b w", w=WINDOWS[p])

        def steps_done(p, pair, stream, k):
            return pair.times(2 * p, STEPS_BEFORE[p] + 2 * k + stream + 1)

        def forgets_done(p, pair, stream, k):
            return pair.times(2 * (p - 1), FORGETS_BEFORE[p] + 2 * (k - 1) + stream + 1)

        def lstm_steps(engine, p):
            with engine.Fori(0, PAIRS[p]) as i:
                pair = Turn(0, i, 1)
                for k in range(p):
                    for stream in (0, 1):
                        yield pair, k, stream

        def slot_exists(g, b, back):
            return 0 <= g.number * GB + b - back < B

        def transfers(turn, later=0):
            par = (turn.number + later) % 2
            return turn.times(8, 8 * later + 16 - 8 * par)

        WT = [("ih", p) for p in range(SKIPS)] + [("hh", p) for p in range(1, SKIPS)]

        def by_head(ap):
            return ap.rearrange("p (h c) -> p h c", h=HEADS)

        def by_graph(ap):
            return ap.rearrange("p (b c) -> p b c", b=GB)

        block = ctx.enter_context(nc.Block())

        @block.sync
        def _(sp):
            for s in counters:
                sp.sem_inc(s, SPARE)
            sp.dma_start(adj_nat[:], adj).then_inc(weights_in, 16)

            def load_x(g):
                if exists(g):
                    sp.wait_ge(ax_made, seen(g.times(1, -1)))
                    sp.dma_start(by_graph(x_tile[:, g.parity()]),
                                 x[bass.ds(g.times(GB), GB)].rearrange("b t d -> t b d")).then_inc(x_in[g.parity()], 16)

            x_turns = group_turns(sp, 0, NG - 1)
            load_x(next(x_turns))
            sp.dma_start(w0[:], Wg0).then_inc(weights_in, 16)
            sp.dma_start(w1[:], Wg1).then_inc(weights_in, 16)
            sp.dma_start(b0_rows[:], bg0.rearrange("(o d) -> o d", o=1).broadcast_to([128, D])).then_inc(weights_in, 16)
            sp.dma_start(b1_rows[:], bg1.rearrange("(o d) -> o d", o=1).broadcast_to([128, D])).then_inc(weights_in, 16)
            sp.dma_start(wqkv[:], Wqkv).then_inc(weights_in, 16)
            sp.dma_start(b_in[:, 0], bih.rearrange("p (g k) -> (p g) k", g=4)).then_inc(weights_in, 16)
            sp.dma_start(b_in[:, 1], bhh.rearrange("p (g k) -> (p g) k", g=4)).then_inc(weights_in, 16)
            sp.dma_start(w_nat[:, 0:4 * BANK].rearrange("k (n d) -> k n d", d=D),
                         Wih.rearrange("p (g k) d -> k (p g) d", g=4)).then_inc(lstm_in, 16)
            sp.dma_start(w_nat[:, 4 * BANK:7 * BANK].rearrange("k (n d) -> k n d", d=D),
                         Whh[1:SKIPS].rearrange("p (g k) d -> k (p g) d", g=4)).then_inc(lstm_in, 16)
            for g in x_turns:
                load_x(g)

            sp.wait_ge(h1_lo, seen(NG))
            for g in turns(sp, -1, 2, NG - 3, NG + 1):
                if exists(g, -1):
                    sp.wait_ge(resid_made, seen(g.times(1, 0)))
                    sp.dma_start(by_graph(x_res[:, (g.number + 1) % 2]),
                                 x[bass.ds(g.times(GB, GB), GB)].rearrange("b t d -> t b d")).then_inc(res_in[(g.number + 1) % 2], 16)
                if exists(g, 2):
                    sp.wait_ge(out_made, seen(g.times(1, -1)))
                    sp.dma_start(out[bass.ds(g.times(GB, -2 * GB), GB)].rearrange("b t d -> t b d"),
                                 by_graph(out_tile[:, g.parity()])).then_inc(stored[g.parity()], 16)
            for parity in (0, 1):
                sp.wait_ge(stored[parity], seen(16 * NG // 2))

        @block.gpsimd
        def _(pool):
            nc.gpsimd.memset(ident[:], 1.0).then_inc(consts_made, 1)
            pool.wait_ge(consts_made, 1)
            nc.gpsimd.affine_select(out=ident[:], in_=ident[:], compare_op=ALU.is_equal, fill=0.0, base=0,
                                    pattern=[[-1, 128]], channel_multiplier=1).then_inc(consts_made, 1)
            nc.gpsimd.memset(minus_half[:], -0.5)
            nc.gpsimd.memset(eps[:], EPS)
            nc.gpsimd.memset(head_mask[:], 0.0).then_inc(consts_made, 1)
            pool.wait_ge(consts_made, 3)
            for h in range(HEADS):
                last = nc.gpsimd.memset(head_mask[HD * h:HD * (h + 1), h:h + 1], 1.0)
            last.then_inc(consts_made, 1)

            def split_h1(g):
                pool.wait_ge(h1_hi, seen(g.times(1, 0)))
                cols = bass.ds(g.times(GC, -GC), GC)
                nc.gpsimd.tensor_tensor(seq_lo[:, cols], h1[:, (g.number - 1) % 2],
                                        seq_hi[:, cols].bitcast(F32), ALU.subtract).then_inc(h1_lo, 1)

            for g in group_turns(pool, 0, NG):
                if exists(g, 1):
                    split_h1(g)
                if g.number == 0:
                    for n, (kind, p) in enumerate(WT):
                        hi, lo = (wih_hi, wih_lo) if kind == "ih" else (whh_hi, whh_lo)
                        pool.wait_ge(wt_hi, n + 1)
                        nc.gpsimd.tensor_tensor(lo[:, p], w_half[:, n % 2], hi[:, p].bitcast(F32),
                                                ALU.subtract).then_inc(wt_lo, 1)

            for p in TILE_GRAPHS:
                for pair, k, stream in lstm_steps(pool, p):
                    pool.wait_ge(state_hi_made, seen(steps_done(p, pair, stream, k)))
                    if k < p - 1:
                        nc.gpsimd.tensor_tensor(shaped(state_lo[:, stream], p), shaped(state[:, stream], p),
                                                shaped(state_hi[:, stream].bitcast(F32), p),
                                                ALU.subtract).then_inc(state_lo_made, 1)
                    else:
                        nc.gpsimd.tensor_tensor(seq_cols(seq_lo, p, pair, stream, k), shaped(state[:, stream], p),
                                                seq_cols(seq_hi.bitcast(F32), p, pair, stream, k),
                                                ALU.subtract).then_inc(state_lo_made, 1)

            pool.wait_ge(state_lo_made, seen(ALL_STEPS))
            nc.gpsimd.memset(v_aug[:], 0.0).then_inc(ones_made, 1)
            pool.wait_ge(ones_made, 1)
            nc.gpsimd.memset(v_aug[:, :, :, :, HD:HD + 1], 1.0).then_inc(ones_made, 1)

            def inverse_deviation(norm, count):
                pool.wait_ge(mom_made[norm], seen(count))
                nc.gpsimd.tensor_tensor(var_eps[:], moments[:, norm, :, 1], eps[:], ALU.add).then_inc(eps_made[norm], 1)
                pool.wait_ge(eps_made[norm], seen(count))
                nc.gpsimd.tensor_tensor(rstd[:, norm], var_eps[:], minus_half[:], ALU.pow).then_inc(rstd_made[norm], 1)

            for g in group_turns(pool, -1, NG):
                for b in range(GB):
                    if b == 0 and exists(g, -1):
                        pool.wait_ge(ht_made, seen(g.times(1, 0)))
                        cols = bass.ds(g.times(GC, GC), GC)
                        nc.gpsimd.tensor_tensor(h_sum[:, (g.number + 1) % 2], seq_hi[:, cols].bitcast(F32),
                                                seq_lo[:, cols].bitcast(F32), ALU.add).then_inc(hsum_made, 1)
                    if b == 1 and exists(g, -1):
                        inverse_deviation(0, g.times(1, 2))
                    if b == 3 and exists(g, -1):
                        pool.wait_ge(consts_made, 4)
                        pool.wait_ge(k_out, seen(g.times(1, 2)))
                        pool.wait_ge(scores_made, seen(g.times(GB, 0)))
                        for h in range(HEADS):
                            last = nc.gpsimd.tensor_scalar(k_exp[:, (g.number + 1) % 2, h], k_t[:, 0],
                                                           head_mask[:, h:h + 1], 1.0, ALU.mult, ALU.mult)
                        last.then_inc(k_spread, 1)
                    if slot_exists(g, b, 2):
                        slot, gp = (b - 2) % GB, g.number - (b < 2)
                        pool.wait_ge(attended_made, seen(g.times(GB, b - 1)))
                        if slot == 0:
                            pool.wait_ge(out_made, seen(g.times(1, -1)))
                        cols = slice(slot * D, (slot + 1) * D)
                        nc.gpsimd.tensor_tensor(y[:, gp % 2, cols], attended[:, b % 2, 0:D],
                                                x1[:, gp % 2, cols], ALU.add).then_inc(y_made, 1)
                    if b == 2 and exists(g, 1):
                        inverse_deviation(1, g.times(1, 0))

        @block.scalar
        def _(act):
            def relu_h1(g):
                act.wait_ge(h1_made, seen(g.times(1, 0)))
                act.wait_ge(h1_lo, seen(g.times(1, -2)))
                nc.scalar.activation(h1[:, (g.number - 1) % 2], bank[:, 7], ACT.Relu, scale=2.0).then_inc(h1_out, 1)

            for g in group_turns(act, 0, NG):
                if exists(g):
                    act.wait_ge(ax_made, seen(g.times(1, 1)))
                    act.wait_ge(h0_made, seen(g.times(1, -1)))
                    nc.scalar.activation(ax_sb[:, g.parity()], bank[:, 4], ACT.Copy).then_inc(ax_out, 1)
                    act.wait_ge(h0_biased, seen(g.times(1, 1)))
                    act.wait_ge(u_made, seen(g.times(1, -1)))
                    nc.scalar.activation(h0[:, g.parity()], h0_pre[:, 0], ACT.Relu).then_inc(h0_out, 1)
                if exists(g, 1):
                    relu_h1(g)
                if g.number == 0:
                    for n in range(len(WT)):
                        act.wait_ge(wt_made, n + 1)
                        act.wait_ge(wt_lo, seen(n - 1))
                        nc.scalar.activation(w_half[:, n % 2], bank[:, n % 2], ACT.Copy, scale=0.5).then_inc(wt_half, 1)

            act.wait_ge(setup_out, 3)
            for p in TILE_GRAPHS:
                for pair, k, stream in lstm_steps(act, p):
                    step = steps_done(p, pair, stream, k)
                    act.wait_ge(state_made, seen(step - 2))
                    for gate in FIRST_STEP if k == 0 else LATER_STEP:
                        done = forgets_done(p, pair, stream, k) if gate == GATE_F else step
                        act.wait_ge(gate_made[gate], seen(done))
                        n = (p - 1) * 4 + gate
                        nc.scalar.activation(gates[:, stream, gate, 0:COLS[p]], bank[:, stream * 4 + gate, 0:COLS[p]],
                                             ACT.Tanh, bias=gate_bias[:, n:n + 1],
                                             scale=1.0 if gate == GATE_G else 0.5).then_inc(gate_active[gate], 1)
                    act.wait_ge(cell_made, seen(step))
                    nc.scalar.activation(tanh_cell[:, stream, 0:COLS[p]], cell[:, stream, 0:COLS[p]],
                                         ACT.Tanh, scale=0.5).then_inc(tanh_made, 1)

            def normalize(norm, dst, src, made):
                for b in range(GB):
                    last = nc.scalar.activation(dst[:, b * D:(b + 1) * D], src[:, b * D:(b + 1) * D], ACT.Identity,
                                                scale=rstd[:, norm, b:b + 1], bias=shift[:, norm, b:b + 1])
                last.then_inc(made, 1)

            for g in group_turns(act, -1, NG):
                nxt = (g.number + 1) % 2
                for b in range(GB):
                    if b == 3 and exists(g, -1):
                        act.wait_ge(k_made, seen(g.times(1, 2)))
                        act.wait_ge(k_spread, seen(g.times(1, 1)))
                        nc.scalar.activation(k_t[:, 0], bank[:, 1], ACT.Copy).then_inc(k_out, 1)
                        act.wait_ge(q_made, seen(g.times(1, 2)))
                        act.wait_ge(scores_made, seen(g.times(GB, 0)))
                        nc.scalar.activation(q_t[:, nxt], bank[:, 2], ACT.Copy, scale=HD ** -0.5).then_inc(q_out, 1)
                    if slot_exists(g, b, 1):
                        act.wait_ge(probt_made, seen(g.times(GB, b)))
                        act.wait_ge(pv_made, seen(g.times(GB, b - 2)))
                        nc.scalar.activation(prob_t[:, (b - 1) % 2], bank[:, 5 + (b - 1) % 2], ACT.Copy).then_inc(probt_out, 1)
                    if b == 2 and exists(g, -1):
                        act.wait_ge(x1t_made, seen(g.times(1, 2)))
                        act.wait_ge(v_made, seen(g.times(1, 0)))
                        nc.scalar.activation(x1_t[:, nxt], bank[:, 0], ACT.Copy).then_inc(x1t_out, 1)
                    if slot_exists(g, b, 0):
                        act.wait_ge(max_made, seen(g.times(GB, b + 1)))
                        act.wait_ge(probt_made, seen(g.times(GB, b - 1)))
                        for h in range(HEADS):
                            last = nc.scalar.activation(by_head(prob[:, b % 2])[:, h], by_head(masked[:, b % 2])[:, h],
                                                        ACT.Exp, bias=neg_max[:, b % 2, h:h + 1])
                        last.then_inc(prob_made, 1)
                    if b == 1 and exists(g, -1):
                        act.wait_ge(shift_made[0], seen(g.times(1, 2)))
                        act.wait_ge(y_made, seen(g.times(GB, 0)))
                        normalize(0, x1[:, nxt], resid[:, nxt], x1_made)
                    if b == 3 and exists(g, 1):
                        act.wait_ge(shift_made[1], seen(g.times(1, 0)))
                        act.wait_ge(stored[nxt], seen(transfers(g, -3)))
                        normalize(1, out_tile[:, nxt], y[:, nxt], out_made)

        @block.vector
        def _(dve):
            def rows_of(p_ap, n):
                return p_ap.rearrange("p (o c) -> p o c", o=1).broadcast_to([128, n, p_ap.shape[1]])

            dve.wait_ge(setup_mm, 1)
            nc.vector.tensor_copy(adj_t[:], bank[:, 0, 0:T]).then_inc(setup_out, 1)
            dve.wait_ge(weights_in, 16 * 8)
            nc.vector.tensor_tensor(b_sum[:], b_in[:, 0], b_in[:, 1], ALU.add).then_inc(mask_step, 1)
            nc.vector.tensor_scalar(mask[:], adj_nat[:], 0.0, MASKED, ALU.is_equal, ALU.mult).then_inc(mask_step, 1)
            dve.wait_ge(setup_mm, 2)
            nc.vector.tensor_copy(b0_term[:], bank[:, 1, 0:T]).then_inc(setup_out, 1)
            dve.wait_ge(setup_mm, 3)
            by_gate = bank[:, 2, 0:SKIPS * 4].rearrange("u (p g) -> u p g", g=4)
            to_gate = gate_bias[:].rearrange("u (p g) -> u p g", g=4)
            nc.vector.tensor_scalar(to_gate[:, :, GATE_I:GATE_G], by_gate[:, :, GATE_I:GATE_G], 0.5, None, ALU.mult)
            nc.vector.tensor_copy(to_gate[:, :, GATE_G], by_gate[:, :, GATE_G])
            nc.vector.tensor_scalar(to_gate[:, :, GATE_O], by_gate[:, :, GATE_O], 0.5, None, ALU.mult).then_inc(setup_out, 1)
            dve.wait_ge(mask_step, 2)
            dve.wait_ge(setup_out, 2)

            for g in group_turns(dve, 0, NG):
                if exists(g):
                    dve.wait_ge(h0_made, seen(g.times(1, 1)))
                    dve.wait_ge(h0_out, seen(g.times(1, 0)))
                    nc.vector.tensor_tensor(by_graph(h0_pre[:, 0]), by_graph(bank[:, 5]), rows_of(b0_term[:], GB),
                                            ALU.add).then_inc(h0_biased, 1)
                if exists(g, 1):
                    dve.wait_ge(u_made, seen(g.times(1, 0)))
                    dve.wait_ge(h1_made, seen(g.times(1, -2)))
                    nc.vector.tensor_tensor(by_graph(u_sb[:, (g.number - 1) % 2]), by_graph(bank[:, 6]), rows_of(b1_rows[:], GB),
                                            ALU.add).then_inc(u_out, 1)
                    dve.wait_ge(h1_out, seen(g.times(1, 0)))
                    nc.vector.tensor_copy(seq_hi[:, bass.ds(g.times(GC, -GC), GC)],
                                          h1[:, (g.number - 1) % 2]).then_inc(h1_hi, 1)
                if g.number == 0:
                    for n, (kind, p) in enumerate(WT):
                        dve.wait_ge(wt_half, seen(n + 1))
                        nc.vector.tensor_copy((wih_hi if kind == "ih" else whh_hi)[:, p], w_half[:, n % 2]).then_inc(wt_hi, 1)

            for p in TILE_GRAPHS:
                c = COLS[p]
                for pair, k, stream in lstm_steps(dve, p):
                    step = steps_done(p, pair, stream, k)
                    new = cell[:, stream, 0:c] if k == 0 else added[:, stream, 0:c]
                    if k:
                        forget = forgets_done(p, pair, stream, k)
                        dve.wait_ge(gate_active[GATE_F], seen(forget))
                        nc.vector.scalar_tensor_tensor(kept[:, stream, 0:c], gates[:, stream, GATE_F, 0:c], 1.0,
                                                       cell[:, stream, 0:c], ALU.add, ALU.mult)
                    dve.wait_ge(gate_active[GATE_I], seen(step))
                    dve.wait_ge(gate_active[GATE_G], seen(step))
                    made = nc.vector.scalar_tensor_tensor(new, gates[:, stream, GATE_I, 0:c], 1.0,
                                                          gates[:, stream, GATE_G, 0:c], ALU.add, ALU.mult)
                    made.then_inc(term_made if k else cell_made, 1)
                    if k:
                        dve.wait_ge(term_made, seen(forget))
                        nc.vector.scalar_tensor_tensor(cell[:, stream, 0:c], kept[:, stream, 0:c], 0.5,
                                                       added[:, stream, 0:c], ALU.mult, ALU.add).then_inc(cell_made, 1)
                    dve.wait_ge(gate_active[GATE_O], seen(step))
                    dve.wait_ge(tanh_made, seen(step))
                    dve.wait_ge(state_lo_made, seen(step - 2))
                    nc.vector.scalar_tensor_tensor(state[:, stream, 0:c], gates[:, stream, GATE_O, 0:c], 1.0,
                                                   tanh_cell[:, stream, 0:c], ALU.add, ALU.mult).then_inc(state_made, 1)
                    dve.wait_ge(state_made, seen(step))
                    into = shaped(state_hi[:, stream], p) if k < p - 1 else seq_cols(seq_hi, p, pair, stream, k)
                    nc.vector.tensor_copy(into, shaped(state[:, stream], p)).then_inc(state_hi_made, 1)

            def moments_of(norm, src, count):
                for b in range(GB):
                    last = nc.vector.bn_stats(stats[:, b], src[:, b * D:(b + 1) * D])
                last.then_inc(bn_made[norm], 1)
                dve.wait_ge(setup_out, 3)
                dve.wait_ge(bn_made[norm], seen(count))
                for b in range(GB):
                    last = nc.vector.bn_aggr(moments[:, norm, b], stats[:, b])
                last.then_inc(mom_made[norm], 1)

            def shift_of(norm, count):
                dve.wait_ge(rstd_made[norm], seen(count))
                nc.vector.scalar_tensor_tensor(shift[:, norm], moments[:, norm, :, 0], -1.0, rstd[:, norm],
                                               ALU.mult, ALU.mult).then_inc(shift_made[norm], 1)

            for g in group_turns(dve, -1, NG):
                nxt = (g.number + 1) % 2
                for b in range(GB):
                    if b == 3 and exists(g, -1):
                        dve.wait_ge(v_made, seen(g.times(1, 2)))
                        dve.wait_ge(pv_made, seen(g.times(GB, 0)))
                        nc.vector.tensor_copy(v_aug[:, nxt, :, :, 0:HD].rearrange("p b h w -> p (b h) w"),
                                              bank[:, 1].rearrange("p (n w) -> p n w", w=HD)).then_inc(v_out, 1)
                    if slot_exists(g, b, 0):
                        dve.wait_ge(scores_made, seen(g.times(GB, b + 1)))
                        dve.wait_ge(prob_made, seen(g.times(GB, b - 1)))
                        nc.vector.tensor_tensor(by_head(masked[:, b % 2]), by_head(bank[:, 3 + b % 2]),
                                                rows_of(mask[:], HEADS), ALU.add).then_inc(masked_made, 1)
                        dve.wait_ge(masked_made, seen(g.times(GB, b + 1)))
                        nc.vector.tensor_reduce(neg_max[:, b % 2], by_head(masked[:, b % 2]), AX.X, ALU.max,
                                                negate=True).then_inc(max_made, 1)
                    if b == 1 and exists(g, -1):
                        shift_of(0, g.times(1, 2))
                    if b == 0 and exists(g, -1):
                        dve.wait_ge(ht_made, seen(g.times(1, 2)))
                        dve.wait_ge(res_in[nxt], transfers(g, 1))
                        dve.wait_ge(x1_made, seen(g.times(1, 0)))
                        nc.vector.scalar_tensor_tensor(resid[:, nxt], bank[:, 0], 0.5, x_res[:, nxt],
                                                       ALU.mult, ALU.add).then_inc(resid_made, 1)
                        dve.wait_ge(resid_made, seen(g.times(1, 2)))
                        moments_of(0, resid[:, nxt], g.times(1, 2))
                    if slot_exists(g, b, 2):
                        m = b % 2
                        dve.wait_ge(pv_made, seen(g.times(GB, b - 1)))
                        weighed = bank[:, 7, (b % 2) * HEADS * VW:(b % 2 + 1) * HEADS * VW].rearrange("p (h w) -> p h w", h=HEADS)
                        nc.vector.reciprocal(rec[:, m], weighed[:, :, HD]).then_inc(rec_made, 1)
                        dve.wait_ge(rec_made, seen(g.times(GB, b - 1)))
                        dve.wait_ge(y_made, seen(g.times(GB, b - 3)))
                        nc.vector.tensor_tensor(attended[:, m, 0:D].rearrange("p (h w) -> p h w", h=HEADS),
                                                weighed[:, :, 0:HD],
                                                rec[:, m].rearrange("p (h o) -> p h o", o=1).broadcast_to([128, HEADS, HD]),
                                                ALU.mult).then_inc(attended_made, 1)
                    if b == 2 and exists(g, 1):
                        dve.wait_ge(y_made, seen(g.times(GB, 0)))
                        moments_of(1, y[:, nxt], g.times(1, 0))
                    if b == 3 and exists(g, 1):
                        shift_of(1, g.times(1, 0))

        @block.tensor
        def _(pe):
            pe.wait_ge(consts_made, 4)
            pe.wait_ge(weights_in, 16 * 8)
            nc.tensor.transpose(bank[:, 0, 0:T], adj_nat[:], ident[:]).then_inc(setup_mm, 1)
            pe.wait_ge(setup_out, 1)
            nc.tensor.matmul(bank[:, 1, 0:T], b0_rows[:], adj_t[:], start=True, stop=True).then_inc(setup_mm, 1)
            pe.wait_ge(mask_step, 1)
            nc.tensor.transpose(bank[:, 2, 0:SKIPS * 4], b_sum[:], ident[0:SKIPS * 4, 0:SKIPS * 4]).then_inc(setup_mm, 1)

            def per_graph(out_bank, stationary, moving, made):
                for b in range(GB):
                    cols = slice(b * 128, (b + 1) * 128)
                    last = nc.tensor.matmul(bank[:, out_bank, cols], stationary[:, cols], moving, start=True, stop=True)
                last.then_inc(made, 1)

            for g in group_turns(pe, 0, NG):
                prev = (g.number - 1) % 2
                if exists(g):
                    pe.wait_ge(x_in[g.parity()], transfers(g))
                    pe.wait_ge(ax_out, seen(g.times(1, 0)))
                    per_graph(4, x_tile[:, g.parity()], adj_t[:], ax_made)
                if exists(g, 1):
                    pe.wait_ge(h0_out, seen(g.times(1, 0)))
                    pe.wait_ge(u_out, seen(g.times(1, -1)))
                    per_graph(6, h0[:, prev], w1[:], u_made)
                if exists(g):
                    pe.wait_ge(ax_out, seen(g.times(1, 1)))
                    pe.wait_ge(h0_biased, seen(g.times(1, 0)))
                    nc.tensor.matmul(bank[:, 5], w0[:], ax_sb[:, g.parity()], start=True, stop=True).then_inc(h0_made, 1)
                if exists(g, 1):
                    pe.wait_ge(u_out, seen(g.times(1, 0)))
                    pe.wait_ge(h1_out, seen(g.times(1, -1)))
                    per_graph(7, u_sb[:, prev], adj_t[:], h1_made)
                if g.number == 0:
                    pe.wait_ge(lstm_in, 32)
                    pe.wait_ge(setup_out, 3)
                    for n in range(len(WT)):
                        if n >= 2:
                            pe.wait_ge(wt_half, seen(n - 1))
                        for gate in range(4):
                            at = (n * 4 + gate) * D
                            last = nc.tensor.transpose(bank[:, n % 2, gate * D:(gate + 1) * D],
                                                       w_nat[:, at:at + D], ident[:])
                        last.then_inc(wt_made, 1)

            def product(dst, hi, lo, x_hi, x_lo, start, stop, lo_ready=None):
                nc.tensor.matmul(dst, hi, x_hi, start=start, stop=False)
                nc.tensor.matmul(dst, lo, x_hi, start=False, stop=False)
                return nc.tensor.matmul(dst, hi, x_lo, start=False, stop=stop)

            pe.wait_ge(wt_lo, seen(len(WT)))
            for p in TILE_GRAPHS:
                for pair, k, stream in lstm_steps(pe, p):
                    step = steps_done(p, pair, stream, k)
                    order = FIRST_STEP if k == 0 else LATER_STEP
                    if k == 0:
                        if p == 1:
                            pe.wait_ge(h1_lo, seen(pair.times(2, stream + 1)))
                            if stream == 1:
                                pe.wait_ge(h1_out, seen(NG))
                        elif p == 2:
                            pe.wait_ge(state_lo_made, seen(pair.times(4, 2 * stream + 2)))
                        elif p == 3:
                            pe.wait_ge(state_lo_made, seen(pair.times(4, STEPS_BEFORE[2] + 3 + stream)))
                        else:
                            pe.wait_ge(state_lo_made, seen(pair.times(12, STEPS_BEFORE[3] + 6 + 6 * stream)))

                    def dst(gate):
                        return shaped(bank[:, stream * 4 + gate], p)

                    for gate in order:
                        if gate == GATE_F:
                            pe.wait_ge(gate_active[gate], seen(forgets_done(p, pair, stream, k) - 2))
                        else:
                            pe.wait_ge(gate_active[gate], seen(step - 2))
                        cols = slice(gate * D, (gate + 1) * D)
                        last = product(dst(gate), wih_hi[:, p - 1, cols], wih_lo[:, p - 1, cols],
                                       seq_cols(seq_hi, p, pair, stream, k), seq_cols(seq_lo, p, pair, stream, k),
                                       True, k == 0)
                        if k == 0:
                            last.then_inc(gate_made[gate], 1)
                    if k:
                        pe.wait_ge(state_lo_made, seen(step - 2))
                        for gate in order:
                            cols = slice(gate * D, (gate + 1) * D)
                            product(dst(gate), whh_hi[:, p - 1, cols], whh_lo[:, p - 1, cols],
                                    shaped(state_hi[:, stream], p), shaped(state_lo[:, stream], p),
                                    False, True).then_inc(gate_made[gate], 1)

            for g in group_turns(pe, -1, NG):
                nxt = (g.number + 1) % 2
                for b in range(GB):
                    if slot_exists(g, b, 0):
                        if b == 0:
                            pe.wait_ge(k_spread, seen(g.times(1, 1)))
                            pe.wait_ge(q_out, seen(g.times(1, 1)))
                        pe.wait_ge(masked_made, seen(g.times(GB, b - 1)))
                        cols = slice(b * T, (b + 1) * T)
                        nc.tensor.matmul(by_head(bank[:, 3 + b % 2]), q_t[:, g.parity(), cols],
                                         k_exp[:, g.parity(), :, cols], start=True, stop=True).then_inc(scores_made, 1)
                    if slot_exists(g, b, 1):
                        m = (b - 1) % 2
                        pe.wait_ge(prob_made, seen(g.times(GB, b)))
                        pe.wait_ge(probt_out, seen(g.times(GB, b - 2)))
                        for h in range(HEADS):
                            last = nc.tensor.transpose(by_head(bank[:, 5 + m])[:, h], by_head(prob[:, m])[:, h], ident[:])
                        last.then_inc(probt_made, 1)
                    if b == 0 and exists(g, -1):
                        pe.wait_ge(hsum_made, seen(g.times(1, 2)))
                        pe.wait_ge(x1t_out, seen(g.times(1, 1)))
                        for n in range(GB):
                            cols = slice(n * T, (n + 1) * T)
                            last = nc.tensor.transpose(bank[:, 0, cols], h_sum[:, nxt, cols], ident[:])
                        last.then_inc(ht_made, 1)
                    if b == 2 and exists(g, -1):
                        pe.wait_ge(x1_made, seen(g.times(1, 2)))
                        pe.wait_ge(resid_made, seen(g.times(1, 2)))
                        for n in range(GB):
                            cols = slice(n * T, (n + 1) * T)
                            last = nc.tensor.transpose(bank[:, 0, cols], x1[:, nxt, cols], ident[:])
                        last.then_inc(x1t_made, 1)
                    if slot_exists(g, b, 2):
                        m, gp = b % 2, (g.number - (b < 2)) % 2
                        slot = (b - 2) % GB
                        pe.wait_ge(probt_out, seen(g.times(GB, b - 1)))
                        if slot == 0:
                            pe.wait_ge(v_out, seen(g.times(1, 1)))
                        pe.wait_ge(attended_made, seen(g.times(GB, b - 2)))
                        for h in range(HEADS):
                            at = (m * HEADS + h) * VW
                            last = nc.tensor.matmul(bank[:, 7, at:at + VW], by_head(prob_t[:, m])[:, h],
                                                    v_aug[:, gp, slot, h], start=True, stop=True)
                        last.then_inc(pv_made, 1)
                    if b == 2 and exists(g, -1):
                        pe.wait_ge(x1t_out, seen(g.times(1, 2)))
                        pe.wait_ge(v_out, seen(g.times(1, 1)))
                        nc.tensor.matmul(bank[:, 1], wqkv[:, D:2 * D], x1_t[:, nxt], start=True, stop=True).then_inc(k_made, 1)
                        pe.wait_ge(q_out, seen(g.times(1, 1)))
                        nc.tensor.matmul(bank[:, 2], wqkv[:, 0:D], x1_t[:, nxt], start=True, stop=True).then_inc(q_made, 1)
                        pe.wait_ge(k_out, seen(g.times(1, 2)))
                        per_graph(1, x1_t[:, nxt], wqkv[:, 2 * D:3 * D], v_made)


_INS = ["x", "adj", "L0_gnn_Wg0", "L0_gnn_bg0", "L0_gnn_Wg1", "L0_gnn_bg1", "L0_gnn_Wih", "L0_gnn_Whh",
        "L0_gnn_bih", "L0_gnn_bhh", "L1_gnn_W"]


def kernel(**inputs):
    import numpy as _np
    import concourse.bacc as _bacc
    from concourse import mybir as _mybir
    from concourse.bass_utils import run_bass_kernel_spmd as _run

    nc = _bacc.Bacc("TRN2", target_bir_lowering=False, num_devices=1)
    arrays, args = {}, []
    for name in _INS:
        a = _np.ascontiguousarray(inputs[name])
        arrays[f"in_{name}"] = a
        args.append(nc.dram_tensor(f"in_{name}", a.shape, _mybir.dt.from_np(a.dtype), kind="ExternalInput").ap())
    out = nc.dram_tensor("out_x", inputs["x"].shape, _mybir.dt.from_np(_np.dtype("float32")), kind="ExternalOutput").ap()
    gnn_lstm_attention(nc, *args, out)
    r = _run(nc, [arrays], core_ids=[0])
    return r.results[0]["out_x"]
```

```python
from contextlib import ExitStack

import concourse.bass as bass
from concourse import mybir



class Turn:

    def __init__(self, number, register=None, stride=0):
        self.number, self.register, self.stride = number, register, stride

    def times(self, per, plus=0):
        fixed = self.number * per + plus
        return fixed if self.register is None else self.register * (self.stride * per) + fixed

    def ring(self, size, later=0):
        return (self.number + later) % size


def turns(engine, first, loop_from, loop_to, last, unroll):
    for n in range(first, loop_from):
        yield Turn(n)
    with engine.Fori(0, (loop_to - loop_from + 1) // unroll) as i:
        for u in range(unroll):
            yield Turn(loop_from + u, i, unroll)
    for n in range(loop_to + 1, last + 1):
        yield Turn(n)


class Step:

    def __init__(self, p, k, stream, start, done, forgets):
        self.p, self.k, self.stream, self.start, self.done, self.forgets = p, k, stream, start, done, forgets
        self.first, self.last = k == 0, k == p - 1


def gnn_lstm_attention(nc, x, adj, Wg0, bg0, Wg1, bg1, Wih, Whh, bih, bhh, Wqkv, out):
    F32, F32R = mybir.dt.float32, mybir.dt.float32r
    ALU, ACT, AX_X = mybir.AluOpType, mybir.ActivationFunctionType, mybir.AxisListType.X

    B, T, D = x.shape
    SKIPS = Wih.shape[0]
    HEADS, HD = 4, D // 4
    EPS = 1e-5
    MASKED = -3e38
    GB = 4
    GC = GB * T
    NG = B // GB
    BANK = 512
    GATE_I, GATE_F, GATE_G, GATE_O = range(4)
    FIRST_STEP = (GATE_I, GATE_G, GATE_O)
    LATER_STEP = (GATE_F, GATE_I, GATE_G, GATE_O)
    VW = 64

    TILE_GRAPHS = {1: 4, 2: 8, 3: 8, 4: 16}
    WINDOWS = {p: T // p for p in TILE_GRAPHS}
    COLS = {p: TILE_GRAPHS[p] * WINDOWS[p] for p in TILE_GRAPHS}
    PAIRS = {p: B // (2 * TILE_GRAPHS[p]) for p in TILE_GRAPHS}
    STEPS_BEFORE, FORGETS_BEFORE, total, forgets = {}, {}, 0, 0
    for p in TILE_GRAPHS:
        STEPS_BEFORE[p], FORGETS_BEFORE[p] = total, forgets
        total += PAIRS[p] * 2 * p
        forgets += PAIRS[p] * 2 * (p - 1)
    ALL_STEPS = total
    PAIR_GROUPS = 2 * TILE_GRAPHS[SKIPS] // GB
    WEIGHT_LOADS = 7

    SPARE = 4

    def seen(n):
        return n + SPARE

    ctx = ExitStack()
    with ctx:
        def sb(name, shape, dt=F32):
            return ctx.enter_context(nc.sbuf_tensor(name, shape, dt))

        def sem(name):
            return ctx.enter_context(nc.semaphore(name))

        counters = []

        def counter(name):
            counters.append(sem(name))
            return counters[-1]

        bank = ctx.enter_context(nc.psum_tensor("bank", [128, 8, BANK], F32))

        seq_hi = sb("seq_hi", [D, B * T], F32R)
        seq_lo = sb("seq_lo", [D, B * T], F32R)
        wih_hi = sb("wih_hi", [D, SKIPS, 4 * D], F32R)
        wih_lo = sb("wih_lo", [D, SKIPS, 4 * D], F32R)
        whh_hi = sb("whh_hi", [D, SKIPS - 1, 4 * D], F32R)
        whh_lo = sb("whh_lo", [D, SKIPS - 1, 4 * D], F32R)
        state_hi = sb("state_hi", [D, 2, BANK], F32R)
        state_lo = sb("state_lo", [D, 2, BANK], F32R)

        ident = sb("ident", [128, 128])
        adj_nat = sb("adj_nat", [T, T])
        adj_t = sb("adj_t", [T, T])
        mask = sb("mask", [T, T])
        w0 = sb("w0", [D, D])
        w1 = sb("w1", [D, D])
        wqkv = sb("wqkv", [D, 3 * D])
        b0_rows = sb("b0_rows", [128, D])
        b1_rows = sb("b1_rows", [128, D])
        b0_term = sb("b0_term", [D, T])
        b_in = sb("b_in", [SKIPS * 4, 2, D])
        b_sum = sb("b_sum", [SKIPS * 4, D])
        gate_bias = sb("gate_bias", [D, SKIPS * 4])
        minus_half = sb("minus_half", [128, GB])
        eps = sb("eps", [128, GB])

        early = sb("early", [128, 28 * BANK])
        late = sb("late", [128, 18 * BANK])

        def part(region, at, n):
            return region[:, at * BANK:(at + n) * BANK].rearrange("p (n c) -> p n c", c=BANK)

        x_tile = part(early, 0, 2)
        ax_sb = part(early, 2, 2)
        h0_pre = part(early, 4, 1)
        h0 = part(early, 5, 2)
        u_sb = part(early, 7, 2)
        h1 = part(early, 9, 2)
        w_nat = early[:, 11 * BANK:18 * BANK]
        w_half = part(early, 18, 2)
        gates = late[:, 0:8 * BANK].rearrange("p (s g c) -> p s g c", s=2, g=4)
        cell = part(late, 8, 2)
        kept = part(late, 10, 2)
        added = part(late, 12, 2)
        tanh_cell = part(late, 14, 2)
        state = part(late, 16, 2)
        x_res = part(early, 0, 1)[:, 0]
        h_sum = part(early, 1, 1)[:, 0]
        resid = part(early, 2, 1)[:, 0]
        x1_t = part(early, 3, 1)[:, 0]
        x1 = part(early, 4, 3)
        q_t = part(early, 7, 3)
        v_aug = early[:, 10 * BANK:16 * BANK].rearrange("p (r b h w) -> p r b h w", r=3, b=GB, h=HEADS)
        k_exp = early[:, 16 * BANK:28 * BANK].rearrange("p (r h c) -> p r h c", r=3, h=HEADS)
        masked = part(late, 0, 2)
        prob = part(late, 2, 2)
        prob_t = part(late, 4, 2)
        y = part(late, 6, 3)
        out_tile = part(late, 9, 1)[:, 0]
        attended = part(late, 10, 1)[:, 0].rearrange("p (n c) -> p n c", c=D)
        stats = sb("stats", [128, GB, 6])
        moments = sb("moments", [128, 2, GB, 2])
        var_eps = sb("var_eps", [128, 2, GB])
        rstd = sb("rstd", [128, 2, GB])
        shift = sb("shift", [128, 2, GB])
        neg_max = sb("neg_max", [128, 2, HEADS])
        rec = sb("rec", [128, 2, HEADS])

        AX, H0, U, H1 = range(4)
        GATES_AT = 4
        TRANSPOSES, K_AND_V, Q, SCORES, PROB_T, WEIGHED = 0, 1, 2, 3, 5, 6

        carrier = sem("carrier")
        adj_in = sem("adj_in")
        weights_in = sem("weights_in")
        lstm_in = sem("lstm_in")
        consts_made = sem("consts_made")
        setup_mm = sem("setup_mm")
        setup_out = sem("setup_out")
        mask_made = sem("mask_made")
        bsum_made = sem("bsum_made")
        wt_made = sem("wt_made")
        wt_half = counter("wt_half")
        wt_hi = sem("wt_hi")
        wt_lo = counter("wt_lo")
        x_in = [sem(f"x_in_{n}") for n in "01"]
        ax_made = counter("ax_made")
        ax_out = counter("ax_out")
        h0_made = counter("h0_made")
        h0_biased = counter("h0_biased")
        h0_out = counter("h0_out")
        u_made = counter("u_made")
        u_out = counter("u_out")
        h1_made = counter("h1_made")
        h1_out = counter("h1_out")
        h1_hi = counter("h1_hi")
        h1_lo = counter("h1_lo")
        gate_made = [counter(f"gate_made_{g}") for g in "ifgo"]
        gate_active = [counter(f"gate_active_{g}") for g in "ifgo"]
        term_made = counter("term_made")
        cell_made = counter("cell_made")
        tanh_made = counter("tanh_made")
        state_made = counter("state_made")
        state_hi_made = counter("state_hi_made")
        state_lo_made = counter("state_lo_made")
        ones_made = sem("ones_made")
        res_in = sem("res_in")
        hsum_made = counter("hsum_made")
        ht_made = counter("ht_made")
        resid_made = counter("resid_made")
        bn_made = [counter(f"bn_made_{norm}") for norm in "12"]
        mom_made = [counter(f"mom_made_{norm}") for norm in "12"]
        eps_made = [counter(f"eps_made_{norm}") for norm in "12"]
        rstd_made = [counter(f"rstd_made_{norm}") for norm in "12"]
        shift_made = [counter(f"shift_made_{norm}") for norm in "12"]
        x1_made = counter("x1_made")
        x1t_made = counter("x1t_made")
        x1t_out = counter("x1t_out")
        k_made = counter("k_made")
        k_spread = counter("k_spread")
        q_made = counter("q_made")
        q_out = counter("q_out")
        v_made = counter("v_made")
        v_out = counter("v_out")
        scores_made = counter("scores_made")
        masked_made = counter("masked_made")
        max_made = counter("max_made")
        prob_made = counter("prob_made")
        probt_made = counter("probt_made")
        probt_out = counter("probt_out")
        weighed_made = counter("weighed_made")
        rec_made = counter("rec_made")
        attended_made = counter("attended_made")
        y_made = counter("y_made")
        out_made = counter("out_made")
        stored = counter("stored")

        def graph_turns(engine):
            return turns(engine, 0, 4, NG - 1, NG + 3, 2)

        def attention_turns(engine):
            return turns(engine, 0, 2, NG - 3, NG + 1, 3)

        def exists(turn, back=0):
            return 0 <= turn.number - back < NG

        def slot_exists(g, b, back):
            return 0 <= g.number * GB + b - back < B

        def ring_back(g, b, back):
            n = g.number * GB + b - back
            return (n // GB) % 3, n % GB

        def seq_cols(seq, s):
            p = s.p
            tile = seq[:, bass.ds(s.start, TILE_GRAPHS[p] * T)]
            if p == 1:
                return tile
            if T % p == 0:
                return tile.rearrange("d (w p) -> d w p", p=p)[:, :, s.k]
            return tile.rearrange("d (b t) -> d b t", t=T)[:, :, s.k:s.k + p * (WINDOWS[p] - 1) + 1:p]

        def shaped(ap, p):
            ap = ap[:, 0:COLS[p]]
            return ap if T % p == 0 else ap.rearrange("d (b w) -> d b w", w=WINDOWS[p])

        def first_lstm_step(g):
            return Step(1, 0, g.ring(2), g.times(GC, -4 * GC), g.times(1, -3), None)

        def step_of(p, pair, k, stream):
            width = TILE_GRAPHS[p] * T
            return Step(p, k, stream, pair.times(2 * width, stream * width),
                        pair.times(2 * p, STEPS_BEFORE[p] + 2 * k + stream + 1),
                        pair.times(2 * (p - 1), FORGETS_BEFORE[p] + 2 * (k - 1) + stream + 1))

        def step_before(s, pair):
            if s.stream == 1:
                return step_of(s.p, pair, s.k, 0)
            if not s.first:
                return step_of(s.p, pair, s.k - 1, 1)
            if pair.number > 0:
                return step_of(s.p, Turn(pair.number - 1, pair.register, pair.stride), s.p - 1, 1)
            return step_of(s.p - 1, Turn(PAIRS[s.p - 1] - 1), s.p - 2, 1) if s.p > 2 else None

        def lstm_pairs(engine, p):
            yield Turn(0)
            with engine.Fori(0, PAIRS[p] - 1) as i:
                yield Turn(1, i, 1)

        def lstm_phase(engine, lstm_step, attention_slot):
            for p in range(2, SKIPS):
                for pair in lstm_pairs(engine, p):
                    for k in range(p):
                        for stream in (0, 1):
                            lstm_step(step_of(p, pair, k, stream), pair)
            for pair in (Turn(0), Turn(1)):
                for k in range(SKIPS):
                    for stream in (0, 1):
                        lstm_step(step_of(SKIPS, pair, k, stream), pair)
                        if pair.number == 1:
                            slot = 2 * k + stream
                            attention_slot(Turn(slot // GB - 2), slot % GB)

        def transfers(turn, later=0):
            return turn.times(8, 8 * later + 16 - 8 * turn.ring(2, later))

        WT = [("ih", p) for p in range(SKIPS)] + [("hh", p) for p in range(1, SKIPS)]

        def lstm_weights(kind, p):
            return (wih_hi[:, p], wih_lo[:, p]) if kind == "ih" else (whh_hi[:, p - 1], whh_lo[:, p - 1])

        def alone(engine):
            engine.sem_inc(carrier, 1)

        def by_head(ap):
            return ap.rearrange("p (h c) -> p h c", h=HEADS)

        def by_graph(ap):
            return ap.rearrange("p (b c) -> p b c", b=GB)

        def of(n, width=T):
            return slice(n * width, (n + 1) * width)

        block = ctx.enter_context(nc.Block())

        @block.sync
        def _(sp):
            sp.dma_start(adj_nat[:], adj).then_inc(adj_in, 16)

            def load_x(g):
                sp.wait_ge(ax_made, seen(g.times(1, -1)))
                sp.dma_start(by_graph(x_tile[:, g.ring(2)]),
                             x[bass.ds(g.times(GB), GB)].rearrange("b t d -> t b d")).then_inc(x_in[g.ring(2)], 16)

            sp.dma_start(by_graph(x_tile[:, 0]), x[0:GB].rearrange("b t d -> t b d")).then_inc(x_in[0], 16)
            sp.dma_start(b0_rows[:], bg0.rearrange("(o d) -> o d", o=1).broadcast_to([128, D])).then_inc(weights_in, 16)
            sp.dma_start(w0[:], Wg0).then_inc(weights_in, 16)
            sp.dma_start(w1[:], Wg1).then_inc(weights_in, 16)
            sp.dma_start(b1_rows[:], bg1.rearrange("(o d) -> o d", o=1).broadcast_to([128, D])).then_inc(weights_in, 16)
            sp.dma_start(b_in[:, 0], bih.rearrange("p (g k) -> (p g) k", g=4)).then_inc(weights_in, 16)
            sp.dma_start(b_in[:, 1], bhh.rearrange("p (g k) -> (p g) k", g=4)).then_inc(weights_in, 16)
            sp.dma_start(wqkv[:], Wqkv).then_inc(weights_in, 16)
            for s in counters:
                sp.sem_inc(s, SPARE)
            load_x(Turn(1))
            sp.dma_start(w_nat[:, 0:4 * BANK].rearrange("k (n d) -> k n d", d=D),
                         Wih.rearrange("p (g k) d -> k (p g) d", g=4)).then_inc(lstm_in, 16)
            sp.dma_start(w_nat[:, 4 * BANK:7 * BANK].rearrange("k (n d) -> k n d", d=D),
                         Whh[1:SKIPS].rearrange("p (g k) d -> k (p g) d", g=4)).then_inc(lstm_in, 16)
            for g in turns(sp, 2, 2, NG - 1, NG - 1, 2):
                load_x(g)

            sp.wait_ge(h1_lo, seen(NG))
            for g in turns(sp, -2, 2, NG - 3, NG + 1, 3):
                if exists(g, -2):
                    sp.wait_ge(resid_made, seen(g.times(1, 2)))
                    sp.dma_start(by_graph(x_res), x[bass.ds(g.times(GB, 2 * GB), GB)].rearrange("b t d -> t b d")).then_inc(res_in, 16)
                if exists(g, 2):
                    sp.wait_ge(out_made, seen(g.times(1, -1)))
                    sp.dma_start(out[bass.ds(g.times(GB, -2 * GB), GB)].rearrange("b t d -> t b d"),
                                 by_graph(out_tile)).then_inc(stored, 16)
            sp.wait_ge(stored, seen(16 * NG))

        @block.gpsimd
        def _(pool):
            nc.gpsimd.memset(ident[:], 1.0).then_inc(consts_made, 1)
            pool.wait_ge(consts_made, 1)
            nc.gpsimd.affine_select(out=ident[:], in_=ident[:], compare_op=ALU.is_equal, fill=0.0, base=0,
                                    pattern=[[-1, 128]], channel_multiplier=1).then_inc(consts_made, 1)
            nc.gpsimd.memset(eps[:], EPS)
            nc.gpsimd.memset(minus_half[:], -0.5)

            def lstm_step(s, pair=None):
                pool.wait_ge(state_hi_made, seen(s.done))
                alone(pool)
                hi, lo = (seq_cols(seq_hi, s), seq_cols(seq_lo, s)) if s.last else (
                    shaped(state_hi[:, s.stream], s.p), shaped(state_lo[:, s.stream], s.p))
                nc.gpsimd.tensor_tensor(lo, shaped(state[:, s.stream], s.p), hi.bitcast(F32),
                                        ALU.subtract).then_inc(state_lo_made, 1)
                if s.p == SKIPS and pair.number == 0:
                    share = 18 * BANK // (2 * SKIPS)
                    at = 10 * BANK + (2 * s.k + s.stream) * share
                    nc.gpsimd.memset(early[:, at:at + share], 0.0).then_inc(ones_made, 1)
                    if s.last and s.stream == 1:
                        pool.wait_ge(ones_made, 2 * SKIPS)
                        nc.gpsimd.memset(v_aug[:, :, :, :, HD:HD + 1], 1.0).then_inc(ones_made, 1)

            for g in graph_turns(pool):
                if exists(g, 3):
                    pool.wait_ge(h1_hi, seen(g.times(1, -2)))
                    alone(pool)
                    cols = bass.ds(g.times(GC, -3 * GC), GC)
                    nc.gpsimd.tensor_tensor(seq_lo[:, cols], h1[:, g.ring(2, -3)],
                                            seq_hi[:, cols].bitcast(F32), ALU.subtract).then_inc(h1_lo, 1)
                if g.number == 2:
                    for n, (kind, p) in enumerate(WT):
                        hi, lo = lstm_weights(kind, p)
                        pool.wait_ge(wt_hi, n + 1)
                        nc.gpsimd.tensor_tensor(lo, w_half[:, n % 2], hi.bitcast(F32), ALU.subtract).then_inc(wt_lo, 1)
                if exists(g, 4):
                    lstm_step(first_lstm_step(g))

            def inverse_deviation(norm, count):
                pool.wait_ge(mom_made[norm], seen(count))
                nc.gpsimd.tensor_tensor(var_eps[:, norm], moments[:, norm, :, 1], eps[:], ALU.add).then_inc(eps_made[norm], 1)
                pool.wait_ge(eps_made[norm], seen(count))
                nc.gpsimd.tensor_tensor(rstd[:, norm], var_eps[:, norm], minus_half[:], ALU.pow).then_inc(rstd_made[norm], 1)

            def normalize(norm, dst, src, made):
                for b in range(GB):
                    last = nc.gpsimd.tensor_scalar(dst[:, of(b)], src[:, of(b)], rstd[:, norm, b:b + 1],
                                                   shift[:, norm, b:b + 1], ALU.mult, ALU.add)
                last.then_inc(made, 1)

            def attention_slot(g, b):
                if b == 0 and exists(g, -2):
                    if g.number == -2:
                        pool.wait_ge(state_lo_made, seen(STEPS_BEFORE[SKIPS] + 2 * SKIPS))
                    elif g.number == PAIR_GROUPS - 2:
                        pool.wait_ge(state_lo_made, seen(ALL_STEPS))
                    pool.wait_ge(ht_made, seen(g.times(1, 2)))
                    alone(pool)
                    cols = bass.ds(g.times(GC, 2 * GC), GC)
                    nc.gpsimd.tensor_tensor(h_sum, seq_hi[:, cols].bitcast(F32),
                                            seq_lo[:, cols].bitcast(F32), ALU.add).then_inc(hsum_made, 1)
                if b == 1 and exists(g, 2):
                    inverse_deviation(1, g.times(1, -1))
                if b == 2 and exists(g, -2):
                    inverse_deviation(0, g.times(1, 3))
                if slot_exists(g, b, 4):
                    ring, slot = ring_back(g, b, 4)
                    pool.wait_ge(attended_made, seen(g.times(GB, b - 3)))
                    nc.gpsimd.tensor_tensor(y[:, ring, of(slot)], attended[:, b % 2],
                                            x1[:, ring, of(slot)], ALU.add).then_inc(y_made, 1)
                if b == 2 and exists(g, 2):
                    pool.wait_ge(shift_made[1], seen(g.times(1, -1)))
                    pool.wait_ge(stored, seen(g.times(16, -32)))
                    alone(pool)
                    normalize(1, out_tile, y[:, g.ring(3, -2)], out_made)
                if b == 3 and exists(g, -2):
                    pool.wait_ge(shift_made[0], seen(g.times(1, 3)))
                    pool.wait_ge(x1t_made, seen(g.times(1, 0)))
                    if g.number >= 1:
                        pool.wait_ge(y_made, seen(g.times(GB, 0)))
                    alone(pool)
                    normalize(0, x1[:, g.ring(3, 2)], resid, x1_made)

            lstm_phase(pool, lstm_step, attention_slot)
            for g in attention_turns(pool):
                for b in range(GB):
                    attention_slot(g, b)

        @block.scalar
        def _(act):
            def activate(s, gate):
                act.wait_ge(gate_made[gate], seen(s.forgets if gate == GATE_F else s.done))
                n = (s.p - 1) * 4 + gate
                nc.scalar.activation(gates[:, s.stream, gate, 0:COLS[s.p]], bank[:, GATES_AT + gate, 0:COLS[s.p]],
                                     ACT.Tanh, bias=gate_bias[:, n:n + 1],
                                     scale=1.0 if gate == GATE_G else 0.5).then_inc(gate_active[gate], 1)

            def tanh_of_cell(s):
                act.wait_ge(cell_made, seen(s.done))
                nc.scalar.activation(tanh_cell[:, s.stream, 0:COLS[s.p]], cell[:, s.stream, 0:COLS[s.p]],
                                     ACT.Tanh, scale=0.5).then_inc(tanh_made, 1)

            def activate_gates(s, before=None):
                if before and not s.first:
                    tanh_of_cell(before)
                act.wait_ge(state_made, seen(s.done - 2))
                for n, gate in enumerate(FIRST_STEP if s.first else LATER_STEP):
                    activate(s, gate)
                    if before and s.first and n == 0:
                        tanh_of_cell(before)

            for g in graph_turns(act):
                if exists(g):
                    act.wait_ge(ax_made, seen(g.times(1, 1)))
                    act.wait_ge(h0_made, seen(g.times(1, -1)))
                    nc.scalar.activation(ax_sb[:, g.ring(2)], bank[:, AX], ACT.Copy).then_inc(ax_out, 1)
                if exists(g, 1):
                    act.wait_ge(h0_biased, seen(g.times(1, 0)))
                    act.wait_ge(u_made, seen(g.times(1, -2)))
                    nc.scalar.activation(h0[:, g.ring(2, -1)], h0_pre[:, 0], ACT.Relu).then_inc(h0_out, 1)
                if exists(g, 3):
                    act.wait_ge(h1_made, seen(g.times(1, -2)))
                    act.wait_ge(h1_lo, seen(g.times(1, -4)))
                    nc.scalar.activation(h1[:, g.ring(2, -3)], bank[:, H1], ACT.Relu, scale=2.0).then_inc(h1_out, 1)
                if g.number == 2:
                    for n in range(len(WT)):
                        act.wait_ge(wt_made, n + 1)
                        act.wait_ge(wt_lo, seen(n - 1))
                        nc.scalar.activation(w_half[:, n % 2], bank[:, 4 + n % 2], ACT.Copy, scale=0.5).then_inc(wt_half, 1)
                    act.wait_ge(setup_out, 3)
                if exists(g, 4):
                    activate_gates(first_lstm_step(g))
                    tanh_of_cell(first_lstm_step(g))

            def attention_slot(g, b):
                if slot_exists(g, b, 1):
                    m = (b - 1) % 2
                    act.wait_ge(max_made, seen(g.times(GB, b)))
                    act.wait_ge(probt_made, seen(g.times(GB, b - 2)))
                    for h in range(HEADS):
                        last = nc.scalar.activation(by_head(prob[:, m])[:, h], by_head(masked[:, m])[:, h],
                                                    ACT.Exp, bias=neg_max[:, m, h:h + 1])
                    last.then_inc(prob_made, 1)
                if slot_exists(g, b, 2):
                    m = b % 2
                    act.wait_ge(probt_made, seen(g.times(GB, b - 1)))
                    act.wait_ge(weighed_made, seen(g.times(GB, b - 3)))
                    nc.scalar.activation(prob_t[:, m], bank[:, PROB_T], ACT.Copy).then_inc(probt_out, 1)
                if b == 0 and exists(g, -1):
                    act.wait_ge(x1t_made, seen(g.times(1, 2)))
                    act.wait_ge(v_made, seen(g.times(1, 1)))
                    nc.scalar.activation(x1_t, bank[:, TRANSPOSES], ACT.Copy).then_inc(x1t_out, 1)
                if b == 2 and exists(g, -1):
                    nxt = g.ring(3, 1)
                    act.wait_ge(k_made, seen(g.times(1, 2)))
                    if g.number >= 2:
                        act.wait_ge(scores_made, seen(g.times(GB, -4)))
                    act.wait_ge(ones_made, 2 * SKIPS + 1)
                    for h in range(HEADS):
                        rows = of(h, HD)
                        last = nc.scalar.activation(k_exp[rows, nxt, h], bank[rows, K_AND_V], ACT.Copy)
                    last.then_inc(k_spread, 1)
                    act.wait_ge(q_made, seen(g.times(1, 2)))
                    nc.scalar.activation(q_t[:, nxt], bank[:, Q], ACT.Copy, scale=HD ** -0.5).then_inc(q_out, 1)

            def lstm_step(s, pair):
                activate_gates(s, step_before(s, pair))

            lstm_phase(act, lstm_step, attention_slot)
            tanh_of_cell(step_of(SKIPS, Turn(1), SKIPS - 1, 1))
            for g in attention_turns(act):
                for b in range(GB):
                    attention_slot(g, b)

        @block.vector
        def _(dve):
            def rows_of(p_ap, n):
                return p_ap.rearrange("p (o c) -> p o c", o=1).broadcast_to([128, n, p_ap.shape[1]])

            dve.wait_ge(setup_mm, 1)
            nc.vector.tensor_copy(adj_t[:], bank[:, 4, 0:T]).then_inc(setup_out, 1)
            dve.wait_ge(adj_in, 16)
            nc.vector.tensor_scalar(mask[:], adj_nat[:], 0.0, MASKED, ALU.is_equal, ALU.mult).then_inc(mask_made, 1)
            dve.wait_ge(weights_in, 16 * WEIGHT_LOADS)
            nc.vector.tensor_tensor(b_sum[:], b_in[:, 0], b_in[:, 1], ALU.add).then_inc(bsum_made, 1)
            dve.wait_ge(setup_mm, 2)
            nc.vector.tensor_copy(b0_term[:], bank[:, 5, 0:T]).then_inc(setup_out, 1)
            dve.wait_ge(setup_mm, 3)
            by_gate = bank[:, 6, 0:SKIPS * 4].rearrange("u (p g) -> u p g", g=4)
            to_gate = gate_bias[:].rearrange("u (p g) -> u p g", g=4)
            nc.vector.tensor_scalar(to_gate[:, :, GATE_I:GATE_G], by_gate[:, :, GATE_I:GATE_G], 0.5, None, ALU.mult)
            nc.vector.tensor_copy(to_gate[:, :, GATE_G], by_gate[:, :, GATE_G])
            nc.vector.tensor_scalar(to_gate[:, :, GATE_O], by_gate[:, :, GATE_O], 0.5, None, ALU.mult).then_inc(setup_out, 1)
            dve.wait_ge(mask_made, 1)
            dve.wait_ge(setup_out, 2)

            def lstm_step(s, pair=None):
                stream, c = s.stream, COLS[s.p]
                new = cell[:, stream, 0:c] if s.first else added[:, stream, 0:c]
                if not s.first:
                    dve.wait_ge(gate_active[GATE_F], seen(s.forgets))
                    nc.vector.scalar_tensor_tensor(kept[:, stream, 0:c], gates[:, stream, GATE_F, 0:c], 1.0,
                                                   cell[:, stream, 0:c], ALU.add, ALU.mult)
                dve.wait_ge(gate_active[GATE_I], seen(s.done))
                dve.wait_ge(gate_active[GATE_G], seen(s.done))
                nc.vector.scalar_tensor_tensor(new, gates[:, stream, GATE_I, 0:c], 1.0, gates[:, stream, GATE_G, 0:c],
                                               ALU.add, ALU.mult).then_inc(cell_made if s.first else term_made, 1)
                if not s.first:
                    dve.wait_ge(term_made, seen(s.forgets))
                    nc.vector.scalar_tensor_tensor(cell[:, stream, 0:c], kept[:, stream, 0:c], 0.5,
                                                   added[:, stream, 0:c], ALU.mult, ALU.add).then_inc(cell_made, 1)
                dve.wait_ge(gate_active[GATE_O], seen(s.done))
                dve.wait_ge(tanh_made, seen(s.done))
                dve.wait_ge(state_lo_made, seen(s.done - 2))
                nc.vector.scalar_tensor_tensor(state[:, stream, 0:c], gates[:, stream, GATE_O, 0:c], 1.0,
                                               tanh_cell[:, stream, 0:c], ALU.add, ALU.mult).then_inc(state_made, 1)
                dve.wait_ge(state_made, seen(s.done))
                alone(dve)
                into = seq_cols(seq_hi, s) if s.last else shaped(state_hi[:, stream], s.p)
                nc.vector.tensor_copy(into, shaped(state[:, stream], s.p)).then_inc(state_hi_made, 1)

            for g in graph_turns(dve):
                if exists(g, 1):
                    dve.wait_ge(h0_made, seen(g.times(1, 0)))
                    dve.wait_ge(h0_out, seen(g.times(1, -1)))
                    nc.vector.tensor_tensor(by_graph(h0_pre[:, 0]), by_graph(bank[:, H0]), rows_of(b0_term[:], GB),
                                            ALU.add).then_inc(h0_biased, 1)
                if exists(g, 2):
                    dve.wait_ge(u_made, seen(g.times(1, -1)))
                    dve.wait_ge(h1_made, seen(g.times(1, -3)))
                    nc.vector.tensor_tensor(by_graph(u_sb[:, g.ring(2, -2)]), by_graph(bank[:, U]), rows_of(b1_rows[:], GB),
                                            ALU.add).then_inc(u_out, 1)
                if exists(g, 3):
                    dve.wait_ge(h1_out, seen(g.times(1, -2)))
                    alone(dve)
                    nc.vector.tensor_copy(seq_hi[:, bass.ds(g.times(GC, -3 * GC), GC)],
                                          h1[:, g.ring(2, -3)]).then_inc(h1_hi, 1)
                if g.number == 2:
                    for n, (kind, p) in enumerate(WT):
                        dve.wait_ge(wt_half, seen(n + 1))
                        nc.vector.tensor_copy(lstm_weights(kind, p)[0], w_half[:, n % 2]).then_inc(wt_hi, 1)
                if exists(g, 4):
                    lstm_step(first_lstm_step(g))

            def moments_of(norm, src, count):
                for b in range(GB):
                    last = nc.vector.bn_stats(stats[:, b], src[:, of(b)])
                last.then_inc(bn_made[norm], 1)
                dve.wait_ge(bn_made[norm], seen(count))
                alone(dve)
                for b in range(GB):
                    last = nc.vector.bn_aggr(moments[:, norm, b], stats[:, b])
                last.then_inc(mom_made[norm], 1)

            def shift_of(norm, count):
                dve.wait_ge(rstd_made[norm], seen(count))
                nc.vector.scalar_tensor_tensor(shift[:, norm], moments[:, norm, :, 0], -1.0, rstd[:, norm],
                                               ALU.mult, ALU.mult).then_inc(shift_made[norm], 1)

            def attention_slot(g, b):
                if b == 3 and exists(g, -2):
                    shift_of(0, g.times(1, 3))
                if slot_exists(g, b, 4):
                    m, done = b % 2, g.times(GB, b - 3)
                    dve.wait_ge(weighed_made, seen(done))
                    weighed = bank[:, WEIGHED + m, 0:HEADS * VW].rearrange("p (h w) -> p h w", h=HEADS)
                    nc.vector.reciprocal(rec[:, m], weighed[:, :, HD]).then_inc(rec_made, 1)
                    dve.wait_ge(rec_made, seen(done))
                    dve.wait_ge(y_made, seen(g.times(GB, b - 5)))
                    nc.vector.tensor_tensor(attended[:, m].rearrange("p (h w) -> p h w", h=HEADS),
                                            weighed[:, :, 0:HD],
                                            rec[:, m].rearrange("p (h o) -> p h o", o=1).broadcast_to([128, HEADS, HD]),
                                            ALU.mult).then_inc(attended_made, 1)
                if slot_exists(g, b, 0):
                    m = b % 2
                    dve.wait_ge(scores_made, seen(g.times(GB, b + 1)))
                    dve.wait_ge(prob_made, seen(g.times(GB, b - 1)))
                    nc.vector.tensor_tensor(by_head(masked[:, m]), by_head(bank[:, SCORES + m]),
                                            rows_of(mask[:], HEADS), ALU.add).then_inc(masked_made, 1)
                    dve.wait_ge(masked_made, seen(g.times(GB, b + 1)))
                    nc.vector.tensor_reduce(neg_max[:, m], by_head(masked[:, m]), AX_X, ALU.max,
                                            negate=True).then_inc(max_made, 1)
                if b == 0 and exists(g, 2):
                    dve.wait_ge(y_made, seen(g.times(GB, -GB)))
                    moments_of(1, y[:, g.ring(3, -2)], g.times(1, -1))
                if b == 1 and exists(g, -2):
                    dve.wait_ge(ht_made, seen(g.times(1, 3)))
                    dve.wait_ge(res_in, g.times(16, 48))
                    dve.wait_ge(x1_made, seen(g.times(1, 2)))
                    nc.vector.scalar_tensor_tensor(resid, bank[:, TRANSPOSES], 0.5, x_res,
                                                   ALU.mult, ALU.add).then_inc(resid_made, 1)
                    dve.wait_ge(resid_made, seen(g.times(1, 3)))
                    moments_of(0, resid, g.times(1, 3))
                if b == 2 and exists(g, 2):
                    shift_of(1, g.times(1, -1))
                if b == 0 and exists(g):
                    dve.wait_ge(v_made, seen(g.times(1, 1)))
                    dve.wait_ge(ones_made, 2 * SKIPS + 1)
                    if g.number >= 1:
                        dve.wait_ge(weighed_made, seen(g.times(GB, -8)))
                    nc.vector.tensor_copy(v_aug[:, g.ring(3), :, :, 0:HD].rearrange("p b h w -> p (b h) w"),
                                          bank[:, K_AND_V].rearrange("p (n w) -> p n w", w=HD)).then_inc(v_out, 1)

            lstm_phase(dve, lstm_step, attention_slot)
            for g in attention_turns(dve):
                for b in range(GB):
                    attention_slot(g, b)

        @block.tensor
        def _(pe):
            pe.wait_ge(consts_made, 2)
            pe.wait_ge(adj_in, 16)
            nc.tensor.transpose(bank[:, 4, 0:T], adj_nat[:], ident[:]).then_inc(setup_mm, 1)

            def per_graph(out_bank, stationary, moving, made):
                for b in range(GB):
                    last = nc.tensor.matmul(bank[:, out_bank, of(b)], stationary[:, of(b)], moving, start=True, stop=True)
                last.then_inc(made, 1)

            def product(dst, hi, lo, x_hi, x_lo, start, stop):
                nc.tensor.matmul(dst, hi, x_hi, start=start, stop=False)
                nc.tensor.matmul(dst, lo, x_hi, start=False, stop=False)
                return nc.tensor.matmul(dst, hi, x_lo, start=False, stop=stop)

            def lstm_step(s, pair=None):
                order = FIRST_STEP if s.first else LATER_STEP
                if s.first:
                    if s.p == 1:
                        pe.wait_ge(h1_lo, seen(s.done))
                    elif s.p == 2:
                        pe.wait_ge(state_lo_made, seen(pair.times(4, 2 * s.stream + 2)))
                    elif s.p == 3:
                        pe.wait_ge(state_lo_made, seen(pair.times(4, STEPS_BEFORE[2] + 3 + s.stream)))
                    else:
                        pe.wait_ge(state_lo_made, seen(pair.times(12, STEPS_BEFORE[3] + 6 + 6 * s.stream)))
                for gate in order:
                    pe.wait_ge(gate_active[gate], seen((s.forgets if gate == GATE_F else s.done) - 1))
                    last = product(shaped(bank[:, GATES_AT + gate], s.p), wih_hi[:, s.p - 1, of(gate, D)],
                                   wih_lo[:, s.p - 1, of(gate, D)], seq_cols(seq_hi, s), seq_cols(seq_lo, s),
                                   True, s.first)
                    if s.first:
                        last.then_inc(gate_made[gate], 1)
                if not s.first:
                    pe.wait_ge(state_lo_made, seen(s.done - 2))
                    for gate in order:
                        product(shaped(bank[:, GATES_AT + gate], s.p), whh_hi[:, s.p - 2, of(gate, D)],
                                whh_lo[:, s.p - 2, of(gate, D)], shaped(state_hi[:, s.stream], s.p),
                                shaped(state_lo[:, s.stream], s.p), False, True).then_inc(gate_made[gate], 1)

            for g in graph_turns(pe):
                if exists(g):
                    if g.number == 0:
                        pe.wait_ge(setup_out, 1)
                    pe.wait_ge(x_in[g.ring(2)], transfers(g))
                    pe.wait_ge(ax_out, seen(g.times(1, 0)))
                    per_graph(AX, x_tile[:, g.ring(2)], adj_t[:], ax_made)
                if g.number == 0:
                    pe.wait_ge(weights_in, 16 * WEIGHT_LOADS)
                    nc.tensor.matmul(bank[:, 5, 0:T], b0_rows[:], adj_t[:], start=True, stop=True).then_inc(setup_mm, 1)
                    pe.wait_ge(bsum_made, 1)
                    nc.tensor.transpose(bank[:, 6, 0:SKIPS * 4], b_sum[:], ident[0:SKIPS * 4, 0:SKIPS * 4]).then_inc(setup_mm, 1)
                if exists(g, 1):
                    pe.wait_ge(ax_out, seen(g.times(1, 0)))
                    pe.wait_ge(h0_biased, seen(g.times(1, -1)))
                    nc.tensor.matmul(bank[:, H0], w0[:], ax_sb[:, g.ring(2, -1)], start=True, stop=True).then_inc(h0_made, 1)
                if exists(g, 2):
                    pe.wait_ge(h0_out, seen(g.times(1, -1)))
                    pe.wait_ge(u_out, seen(g.times(1, -2)))
                    per_graph(U, h0[:, g.ring(2, -2)], w1[:], u_made)
                if exists(g, 3):
                    pe.wait_ge(u_out, seen(g.times(1, -2)))
                    pe.wait_ge(h1_out, seen(g.times(1, -3)))
                    per_graph(H1, u_sb[:, g.ring(2, -3)], adj_t[:], h1_made)
                if g.number == 2:
                    pe.wait_ge(lstm_in, 32)
                    pe.wait_ge(setup_out, 3)
                    for n in range(len(WT)):
                        if n >= 2:
                            pe.wait_ge(wt_half, seen(n - 1))
                        for gate in range(4):
                            last = nc.tensor.transpose(bank[:, 4 + n % 2, of(gate, D)],
                                                       w_nat[:, of(n * 4 + gate, D)], ident[:])
                        last.then_inc(wt_made, 1)
                if exists(g, 4):
                    if g.number == 4:
                        pe.wait_ge(wt_lo, seen(len(WT)))
                    lstm_step(first_lstm_step(g))

            def attention_slot(g, b):
                if slot_exists(g, b, 0):
                    m, now = b % 2, g.ring(3)
                    if b == 0:
                        pe.wait_ge(k_spread, seen(g.times(1, 1)))
                        pe.wait_ge(q_out, seen(g.times(1, 1)))
                    pe.wait_ge(masked_made, seen(g.times(GB, b - 1)))
                    nc.tensor.matmul(by_head(bank[:, SCORES + m]), q_t[:, now, of(b)],
                                     k_exp[:, now, :, of(b)], start=True, stop=True).then_inc(scores_made, 1)
                if slot_exists(g, b, 2):
                    m = b % 2
                    pe.wait_ge(prob_made, seen(g.times(GB, b - 1)))
                    pe.wait_ge(probt_out, seen(g.times(GB, b - 2)))
                    for h in range(HEADS):
                        last = nc.tensor.transpose(by_head(bank[:, PROB_T])[:, h], by_head(prob[:, m])[:, h], ident[:])
                    last.then_inc(probt_made, 1)
                if b == 0 and exists(g, -1):
                    pe.wait_ge(x1_made, seen(g.times(1, 2)))
                    pe.wait_ge(resid_made, seen(g.times(1, 2)))
                    for n in range(GB):
                        last = nc.tensor.transpose(bank[:, TRANSPOSES, of(n)], x1[:, g.ring(3, 1), of(n)], ident[:])
                    last.then_inc(x1t_made, 1)
                if b == 1 and exists(g, -2):
                    pe.wait_ge(hsum_made, seen(g.times(1, 3)))
                    pe.wait_ge(x1t_out, seen(g.times(1, 2)))
                    for n in range(GB):
                        last = nc.tensor.transpose(bank[:, TRANSPOSES, of(n)], h_sum[:, of(n)], ident[:])
                    last.then_inc(ht_made, 1)
                if slot_exists(g, b, 3):
                    ring, slot = ring_back(g, b, 3)
                    m = (b - 3) % 2
                    pe.wait_ge(probt_out, seen(g.times(GB, b - 2)))
                    if slot == 0:
                        pe.wait_ge(v_out, seen(g.times(1, 1)))
                    pe.wait_ge(attended_made, seen(g.times(GB, b - 4)))
                    for h in range(HEADS):
                        nc_last = nc.tensor.matmul(bank[:, WEIGHED + m, of(h, VW)], by_head(prob_t[:, m])[:, h],
                                                   v_aug[:, ring, slot, h], start=True, stop=True)
                    nc_last.then_inc(weighed_made, 1)
                if b == 1 and exists(g, -1):
                    pe.wait_ge(x1t_out, seen(g.times(1, 2)))
                    pe.wait_ge(v_out, seen(g.times(1, 1)))
                    nc.tensor.matmul(bank[:, K_AND_V], wqkv[:, of(1, D)], x1_t, start=True, stop=True).then_inc(k_made, 1)
                    pe.wait_ge(q_out, seen(g.times(1, 1)))
                    nc.tensor.matmul(bank[:, Q], wqkv[:, of(0, D)], x1_t, start=True, stop=True).then_inc(q_made, 1)
                if b == 3 and exists(g, -1):
                    pe.wait_ge(k_spread, seen(g.times(1, 2)))
                    per_graph(K_AND_V, x1_t, wqkv[:, of(2, D)], v_made)

            lstm_phase(pe, lstm_step, attention_slot)
            for g in attention_turns(pe):
                for b in range(GB):
                    attention_slot(g, b)


_INS = ["x", "adj", "L0_gnn_Wg0", "L0_gnn_bg0", "L0_gnn_Wg1", "L0_gnn_bg1", "L0_gnn_Wih", "L0_gnn_Whh",
        "L0_gnn_bih", "L0_gnn_bhh", "L1_gnn_W"]


def kernel(**inputs):
    import numpy as _np
    import concourse.bacc as _bacc
    from concourse import mybir as _mybir
    from concourse.bass_utils import run_bass_kernel_spmd as _run

    nc = _bacc.Bacc("TRN2", target_bir_lowering=False, num_devices=1)
    arrays, args = {}, []
    for name in _INS:
        a = _np.ascontiguousarray(inputs[name])
        arrays[f"in_{name}"] = a
        args.append(nc.dram_tensor(f"in_{name}", a.shape, _mybir.dt.from_np(a.dtype), kind="ExternalInput").ap())
    out = nc.dram_tensor("out_x", inputs["x"].shape, _mybir.dt.from_np(_np.dtype("float32")), kind="ExternalOutput").ap()
    gnn_lstm_attention(nc, *args, out)
    r = _run(nc, [arrays], core_ids=[0])
    return r.results[0]["out_x"]
```

```python
from contextlib import ExitStack

import concourse.bass as bass
from concourse import mybir



class Turn:

    def __init__(self, number, register=None, stride=0):
        self.number, self.register, self.stride = number, register, stride

    def times(self, per, plus=0):
        fixed = self.number * per + plus
        return fixed if self.register is None else self.register * (self.stride * per) + fixed

    def ring(self, size, later=0):
        return (self.number + later) % size


def turns(engine, first, loop_from, loop_to, last, unroll):
    for n in range(first, loop_from):
        yield Turn(n)
    with engine.Fori(0, (loop_to - loop_from + 1) // unroll) as i:
        for u in range(unroll):
            yield Turn(loop_from + u, i, unroll)
    for n in range(loop_to + 1, last + 1):
        yield Turn(n)


class Step:

    def __init__(self, p, k, stream, start, done, forgets):
        self.p, self.k, self.stream, self.start, self.done, self.forgets = p, k, stream, start, done, forgets
        self.first, self.last = k == 0, k == p - 1


def gnn_lstm_attention(nc, x, adj, Wg0, bg0, Wg1, bg1, Wih, Whh, bih, bhh, Wqkv, out):
    F32, F32R = mybir.dt.float32, mybir.dt.float32r
    ALU, ACT, AX_X = mybir.AluOpType, mybir.ActivationFunctionType, mybir.AxisListType.X

    B, T, D = x.shape
    SKIPS = Wih.shape[0]
    HEADS, HD = 4, D // 4
    EPS = 1e-5
    MASKED = -3e38
    GB = 4
    GC = GB * T
    NG = B // GB
    BANK = 512
    GATE_I, GATE_F, GATE_G, GATE_O = range(4)
    FIRST_STEP = (GATE_I, GATE_G, GATE_O)
    LATER_STEP = (GATE_F, GATE_I, GATE_G, GATE_O)
    VW = 64

    TILE_GRAPHS = {1: 4, 2: 8, 3: 8, 4: 16}
    WINDOWS = {p: T // p for p in TILE_GRAPHS}
    COLS = {p: TILE_GRAPHS[p] * WINDOWS[p] for p in TILE_GRAPHS}
    PAIRS = {p: B // (2 * TILE_GRAPHS[p]) for p in TILE_GRAPHS}
    STEPS_BEFORE, FORGETS_BEFORE, total, forgets = {}, {}, 0, 0
    for p in TILE_GRAPHS:
        STEPS_BEFORE[p], FORGETS_BEFORE[p] = total, forgets
        total += PAIRS[p] * 2 * p
        forgets += PAIRS[p] * 2 * (p - 1)
    ALL_STEPS = total
    PAIR_GROUPS = 2 * TILE_GRAPHS[SKIPS] // GB
    WEIGHT_LOADS = 7

    SPARE = 4

    def seen(n):
        return n + SPARE

    ctx = ExitStack()
    with ctx:
        def sb(name, shape, dt=F32):
            return ctx.enter_context(nc.sbuf_tensor(name, shape, dt))

        def sem(name):
            return ctx.enter_context(nc.semaphore(name))

        counters = []

        def counter(name):
            counters.append(sem(name))
            return counters[-1]

        bank = ctx.enter_context(nc.psum_tensor("bank", [128, 8, BANK], F32))

        seq_hi = sb("seq_hi", [D, B * T], F32R)
        seq_lo = sb("seq_lo", [D, B * T], F32R)
        wih_hi = sb("wih_hi", [D, SKIPS, 4 * D], F32R)
        wih_lo = sb("wih_lo", [D, SKIPS, 4 * D], F32R)
        whh_hi = sb("whh_hi", [D, SKIPS - 1, 4 * D], F32R)
        whh_lo = sb("whh_lo", [D, SKIPS - 1, 4 * D], F32R)
        state_hi = sb("state_hi", [D, 2, BANK], F32R)
        state_lo = sb("state_lo", [D, 2, BANK], F32R)

        ident = sb("ident", [128, 128])
        adj_nat = sb("adj_nat", [T, T])
        adj_t = sb("adj_t", [T, T])
        mask = sb("mask", [T, T])
        w0 = sb("w0", [D, D])
        w1 = sb("w1", [D, D])
        wqkv = sb("wqkv", [D, 3 * D])
        wqk_hi = sb("wqk_hi", [D, 2 * D], F32R)
        wqk_lo = sb("wqk_lo", [D, 2 * D], F32R)
        x1t_hi = sb("x1t_hi", [D, GC], F32R)
        x1t_lo = sb("x1t_lo", [D, GC], F32R)
        b0_rows = sb("b0_rows", [128, D])
        b1_rows = sb("b1_rows", [128, D])
        b0_term = sb("b0_term", [D, T])
        b_in = sb("b_in", [SKIPS * 4, 2, D])
        b_sum = sb("b_sum", [SKIPS * 4, D])
        gate_bias = sb("gate_bias", [D, SKIPS * 4])
        minus_half = sb("minus_half", [128, GB])
        eps = sb("eps", [128, GB])

        early = sb("early", [128, 28 * BANK])
        late = sb("late", [128, 18 * BANK])

        def part(region, at, n):
            return region[:, at * BANK:(at + n) * BANK].rearrange("p (n c) -> p n c", c=BANK)

        x_tile = part(early, 0, 2)
        ax_sb = part(early, 2, 2)
        h0_pre = part(early, 4, 1)
        h0 = part(early, 5, 2)
        u_sb = part(early, 7, 2)
        h1 = part(early, 9, 2)
        w_nat = early[:, 11 * BANK:18 * BANK]
        w_half = part(early, 18, 7)
        gates = late[:, 0:8 * BANK].rearrange("p (s g c) -> p s g c", s=2, g=4)
        cell = part(late, 8, 2)
        kept = part(late, 10, 2)
        added = part(late, 12, 2)
        tanh_cell = part(late, 14, 2)
        state = part(late, 16, 2)
        x_res = part(early, 0, 1)[:, 0]
        h_sum = part(early, 1, 1)[:, 0]
        resid = part(early, 2, 1)[:, 0]
        x1_t = part(early, 3, 1)[:, 0]
        x1 = part(early, 4, 3)
        q_t = part(early, 7, 3)
        v_aug = early[:, 10 * BANK:16 * BANK].rearrange("p (r b h w) -> p r b h w", r=3, b=GB, h=HEADS)
        k_exp = early[:, 16 * BANK:28 * BANK].rearrange("p (r h c) -> p r h c", r=3, h=HEADS)
        masked = part(late, 0, 2)
        prob = part(late, 2, 2)
        prob_t = part(late, 4, 2)
        y = part(late, 6, 3)
        attended = part(late, 9, 1)[:, 0].rearrange("p (n c) -> p n c", c=D)
        out_tile = part(late, 11, 3)
        stats = sb("stats", [128, GB, 6])
        moments = sb("moments", [128, 2, GB, 2])
        var_eps = sb("var_eps", [128, 2, GB])
        rstd = sb("rstd", [128, 2, GB])
        shift = sb("shift", [128, 2, GB])
        neg_max = sb("neg_max", [128, 2, HEADS])
        rec = sb("rec", [128, 2, HEADS])

        LAST_SHARE = range(GB - 1, GB)

        AX, H0, U, H1 = range(4)
        GATES_AT = 4
        TRANSPOSES, K_AND_V, Q, SCORES, PROB_T, WEIGHED = 0, 1, 2, 3, 5, 6

        carrier = sem("carrier")
        adj_in = sem("adj_in")
        weights_in = sem("weights_in")
        first_lstm_in = sem("first_lstm_in")
        lstm_in = sem("lstm_in")
        consts_made = sem("consts_made")
        setup_mm = sem("setup_mm")
        setup_out = sem("setup_out")
        mask_made = sem("mask_made")
        bsum_made = sem("bsum_made")
        wt_made = sem("wt_made")
        wt_half = counter("wt_half")
        wt_hi = sem("wt_hi")
        wt_lo = counter("wt_lo")
        x_in = [sem(f"x_in_{n}") for n in "01"]
        ax_made = counter("ax_made")
        ax_out = counter("ax_out")
        h0_made = counter("h0_made")
        h0_biased = counter("h0_biased")
        h0_out = counter("h0_out")
        u_made = counter("u_made")
        u_out = counter("u_out")
        h1_made = counter("h1_made")
        h1_out = counter("h1_out")
        h1_hi = counter("h1_hi")
        h1_lo = counter("h1_lo")
        gate_made = [counter(f"gate_made_{g}") for g in "ifgo"]
        gate_active = [counter(f"gate_active_{g}") for g in "ifgo"]
        term_made = counter("term_made")
        cell_made = counter("cell_made")
        tanh_made = counter("tanh_made")
        state_made = counter("state_made")
        state_hi_made = counter("state_hi_made")
        state_lo_made = counter("state_lo_made")
        ones_made = sem("ones_made")
        res_in = sem("res_in")
        hsum_made = counter("hsum_made")
        ht_made = counter("ht_made")
        resid_made = counter("resid_made")
        bn_made = [counter(f"bn_made_{norm}") for norm in "12"]
        mom_made = [counter(f"mom_made_{norm}") for norm in "12"]
        eps_made = [counter(f"eps_made_{norm}") for norm in "12"]
        rstd_made = [counter(f"rstd_made_{norm}") for norm in "12"]
        shift_made = [counter(f"shift_made_{norm}") for norm in "12"]
        x1_made = counter("x1_made")
        x1t_made = counter("x1t_made")
        x1t_out = counter("x1t_out")
        x1t_hi_made = counter("x1t_hi_made")
        x1t_lo_made = counter("x1t_lo_made")
        wqk_hi_made = sem("wqk_hi_made")
        wqk_lo_made = sem("wqk_lo_made")
        k_made = counter("k_made")
        k_spread = counter("k_spread")
        q_made = counter("q_made")
        q_out = counter("q_out")
        v_made = counter("v_made")
        v_out = counter("v_out")
        scores_made = counter("scores_made")
        masked_made = counter("masked_made")
        max_made = counter("max_made")
        prob_made = counter("prob_made")
        probt_made = counter("probt_made")
        probt_out = counter("probt_out")
        weighed_made = counter("weighed_made")
        rec_made = counter("rec_made")
        attended_made = counter("attended_made")
        y_made = counter("y_made")
        out_made = counter("out_made")
        last_out = sem("last_out")
        stored = [counter(f"stored_{n}") for n in "012"]

        def graph_turns(engine):
            return turns(engine, 0, 6, NG - 1, NG + 3, 2)

        def attention_turns(engine):
            return turns(engine, 0, 2, NG - 3, NG + 1, 3)

        def exists(turn, back=0):
            return 0 <= turn.number - back < NG

        def slot_exists(g, b, back):
            return 0 <= g.number * GB + b - back < B

        def ring_back(g, b, back):
            n = g.number * GB + b - back
            return (n // GB) % 3, n % GB

        def seq_cols(seq, s):
            p = s.p
            tile = seq[:, bass.ds(s.start, TILE_GRAPHS[p] * T)]
            if p == 1:
                return tile
            if T % p == 0:
                return tile.rearrange("d (w p) -> d w p", p=p)[:, :, s.k]
            return tile.rearrange("d (b t) -> d b t", t=T)[:, :, s.k:s.k + p * (WINDOWS[p] - 1) + 1:p]

        def shaped(ap, p):
            ap = ap[:, 0:COLS[p]]
            return ap if T % p == 0 else ap.rearrange("d (b w) -> d b w", w=WINDOWS[p])

        def first_lstm_step(g, back=4):
            return Step(1, 0, g.ring(2, -back), g.times(GC, -back * GC), g.times(1, 1 - back), None)

        def step_of(p, pair, k, stream):
            width = TILE_GRAPHS[p] * T
            return Step(p, k, stream, pair.times(2 * width, stream * width),
                        pair.times(2 * p, STEPS_BEFORE[p] + 2 * k + stream + 1),
                        pair.times(2 * (p - 1), FORGETS_BEFORE[p] + 2 * (k - 1) + stream + 1))

        def step_before(s, pair):
            if s.stream == 1:
                return step_of(s.p, pair, s.k, 0)
            if not s.first:
                return step_of(s.p, pair, s.k - 1, 1)
            if pair.number > 0:
                return step_of(s.p, Turn(pair.number - 1, pair.register, pair.stride), s.p - 1, 1)
            return step_of(s.p - 1, Turn(PAIRS[s.p - 1] - 1), s.p - 2, 1) if s.p > 2 else None

        def lstm_pairs(engine, p):
            yield Turn(0)
            with engine.Fori(0, PAIRS[p] - 1) as i:
                yield Turn(1, i, 1)

        SLOTS_AFTER = {0: [0], 2: [1], 3: [2, 3], 5: [4], 6: [5, 6, 7]}
        PE_SLOTS_AFTER = {**SLOTS_AFTER, 6: [5, 6], 7: [7]}
        POOL_SLOTS_AFTER = {0: [0], 2: [1], 3: [2, 3, 4], 5: [5], 6: [6, 7, 8]}

        def lstm_phase(engine, lstm_step, attention_slot, slots_after=SLOTS_AFTER):
            for p in range(2, SKIPS):
                for pair in lstm_pairs(engine, p):
                    for k in range(p):
                        for stream in (0, 1):
                            lstm_step(step_of(p, pair, k, stream), pair)
            for pair in (Turn(0), Turn(1)):
                for k in range(SKIPS):
                    for stream in (0, 1):
                        lstm_step(step_of(SKIPS, pair, k, stream), pair)
                        if pair.number == 1:
                            for slot in slots_after.get(2 * k + stream, []):
                                attention_slot(Turn(slot // GB - 2), slot % GB)

        def transfers(turn, later=0):
            return turn.times(8, 8 * later + 16 - 8 * turn.ring(2, later))

        def stores_before(turn):
            stores = 16 * ((turn.number - 2) // 3)
            return stores if turn.register is None else turn.register * (16 * turn.stride // 3) + stores

        WT = [("ih", 0)] + [(kind, p) for p in range(1, SKIPS) for kind in ("ih", "hh")]
        WT_TURN = {2: [0], NG: [1], NG + 1: [2], NG + 2: [3, 4], NG + 3: [5, 6]}
        WT_BANK = (4, AX, AX, H0, AX, H0, U)

        def weights_now(turn):
            return WT_TURN.get(turn.number, [])

        def matrix_at(n):
            kind, p = WT[n]
            return 4 * (p if kind == "ih" else SKIPS + p - 1)

        def lstm_weights(kind, p):
            return (wih_hi[:, p], wih_lo[:, p]) if kind == "ih" else (whh_hi[:, p - 1], whh_lo[:, p - 1])

        def alone(engine):
            engine.sem_inc(carrier, 1)

        def by_head(ap):
            return ap.rearrange("p (h c) -> p h c", h=HEADS)

        def by_graph(ap):
            return ap.rearrange("p (b c) -> p b c", b=GB)

        def of(n, width=T):
            return slice(n * width, (n + 1) * width)

        block = ctx.enter_context(nc.Block())

        @block.sync
        def _(sp):
            sp.dma_start(adj_nat[:], adj).then_inc(adj_in, 16)

            def load_x(g):
                sp.wait_ge(ax_made, seen(g.times(1, -1)))
                sp.dma_start(by_graph(x_tile[:, g.ring(2)]),
                             x[bass.ds(g.times(GB), GB)].rearrange("b t d -> t b d")).then_inc(x_in[g.ring(2)], 16)

            sp.dma_start(by_graph(x_tile[:, 0]), x[0:GB].rearrange("b t d -> t b d")).then_inc(x_in[0], 16)
            sp.dma_start(by_graph(x_tile[:, 1]), x[GB:2 * GB].rearrange("b t d -> t b d")).then_inc(x_in[1], 16)
            sp.dma_start(w0[:], Wg0).then_inc(weights_in, 16)
            sp.dma_start(b0_rows[:], bg0.rearrange("(o d) -> o d", o=1).broadcast_to([128, D])).then_inc(weights_in, 16)
            load_x(Turn(2))
            sp.dma_start(w_nat[:, 0:BANK].rearrange("k (g d) -> k g d", d=D),
                         Wih[0].rearrange("(g k) d -> k g d", g=4)).then_inc(first_lstm_in, 16)
            load_x(Turn(3))
            sp.dma_start(w_nat[:, BANK:4 * BANK].rearrange("k (n d) -> k n d", d=D),
                         Wih[1:SKIPS].rearrange("p (g k) d -> k (p g) d", g=4)).then_inc(lstm_in, 16)
            sp.dma_start(w_nat[:, 4 * BANK:7 * BANK].rearrange("k (n d) -> k n d", d=D),
                         Whh[1:SKIPS].rearrange("p (g k) d -> k (p g) d", g=4)).then_inc(lstm_in, 16)
            for g in turns(sp, 4, 4, NG - 1, NG - 1, 2):
                load_x(g)

            sp.wait_ge(h1_lo, seen(NG))
            for g in turns(sp, -2, 2, NG - 3, NG + 1, 3):
                if exists(g, -2):
                    sp.wait_ge(resid_made, seen(g.times(1, 2)))
                    sp.dma_start(by_graph(x_res), x[bass.ds(g.times(GB, 2 * GB), GB)].rearrange("b t d -> t b d")).then_inc(res_in, 16)
                if exists(g, 2):
                    sp.wait_ge(out_made, seen(g.times(1, -1)))
                    if g.number >= NG:
                        sp.wait_ge(last_out, g.number + 1 - NG)
                    sp.dma_start(out[bass.ds(g.times(GB, -2 * GB), GB)].rearrange("b t d -> t b d"),
                                 by_graph(out_tile[:, g.ring(3, -2)])).then_inc(stored[g.ring(3, -2)], 16)
            for n in range(3):
                sp.wait_ge(stored[n], seen(16 * len(range(n, NG, 3))))

        @block.gpsimd
        def _(pool):
            nc.gpsimd.memset(ident[:], 1.0).then_inc(consts_made, 1)
            pool.wait_ge(consts_made, 1)
            nc.gpsimd.affine_select(out=ident[:], in_=ident[:], compare_op=ALU.is_equal, fill=0.0, base=0,
                                    pattern=[[-1, 128]], channel_multiplier=1).then_inc(consts_made, 1)
            for s in counters:
                pool.sem_inc(s, SPARE)
            nc.gpsimd.memset(eps[:], EPS)
            nc.gpsimd.memset(minus_half[:], -0.5)

            def lstm_step(s, pair=None):
                pool.wait_ge(state_hi_made, seen(s.done))
                alone(pool)
                hi, lo = (seq_cols(seq_hi, s), seq_cols(seq_lo, s)) if s.last else (
                    shaped(state_hi[:, s.stream], s.p), shaped(state_lo[:, s.stream], s.p))
                nc.gpsimd.tensor_tensor(lo, shaped(state[:, s.stream], s.p), hi.bitcast(F32),
                                        ALU.subtract).then_inc(state_lo_made, 1)
                if s.p == SKIPS and pair.number == 0:
                    share = 18 * BANK // (2 * SKIPS)
                    at = 10 * BANK + (2 * s.k + s.stream) * share
                    nc.gpsimd.memset(early[:, at:at + share], 0.0).then_inc(ones_made, 1)
                    if s.last and s.stream == 1:
                        pool.wait_ge(ones_made, 2 * SKIPS)
                        nc.gpsimd.memset(v_aug[:, :, :, :, HD:HD + 1], 1.0).then_inc(ones_made, 1)

            pool.wait_ge(wqk_hi_made, 1)
            nc.gpsimd.tensor_tensor(wqk_lo[:], wqkv[:, 0:2 * D], wqk_hi[:].bitcast(F32), ALU.subtract).then_inc(wqk_lo_made, 1)

            def weights_lo(n):
                hi, lo = lstm_weights(*WT[n])
                pool.wait_ge(wt_hi, n + 1)
                nc.gpsimd.tensor_tensor(lo, w_half[:, n], hi.bitcast(F32), ALU.subtract).then_inc(wt_lo, 1)

            for g in graph_turns(pool):
                if exists(g, 3):
                    pool.wait_ge(h1_hi, seen(g.times(1, -2)))
                    alone(pool)
                    cols = bass.ds(g.times(GC, -3 * GC), GC)
                    nc.gpsimd.tensor_tensor(seq_lo[:, cols], h1[:, g.ring(2, -3)],
                                            seq_hi[:, cols].bitcast(F32), ALU.subtract).then_inc(h1_lo, 1)
                for n in weights_now(g):
                    weights_lo(n)
                if exists(g, 4):
                    lstm_step(first_lstm_step(g))

            def inverse_deviation(norm, count):
                pool.wait_ge(mom_made[norm], seen(count))
                nc.gpsimd.tensor_tensor(var_eps[:, norm], moments[:, norm, :, 1], eps[:], ALU.add).then_inc(eps_made[norm], 1)
                pool.wait_ge(eps_made[norm], seen(count))
                nc.gpsimd.tensor_tensor(rstd[:, norm], var_eps[:, norm], minus_half[:], ALU.pow).then_inc(rstd_made[norm], 1)

            def normalize(norm, dst, src, made, graphs=range(GB)):
                for b in graphs:
                    last = nc.gpsimd.tensor_scalar(dst[:, of(b)], src[:, of(b)], rstd[:, norm, b:b + 1],
                                                   shift[:, norm, b:b + 1], ALU.mult, ALU.add)
                if made:
                    last.then_inc(made, 1)

            def attention_slot(g, b):
                if b == 1 and exists(g, -1):
                    pool.wait_ge(x1t_hi_made, seen(g.times(1, 2)))
                    pool.wait_ge(q_made, seen(g.times(1, 1)))
                    alone(pool)
                    nc.gpsimd.tensor_tensor(x1t_lo[:], x1_t, x1t_hi[:].bitcast(F32), ALU.subtract).then_inc(x1t_lo_made, 1)
                if b == 0 and exists(g, -2):
                    if g.number == -2:
                        pool.wait_ge(state_lo_made, seen(STEPS_BEFORE[SKIPS] + 2 * SKIPS))
                    elif g.number == PAIR_GROUPS - 2:
                        pool.wait_ge(state_lo_made, seen(ALL_STEPS))
                    pool.wait_ge(ht_made, seen(g.times(1, 2)))
                    alone(pool)
                    cols = bass.ds(g.times(GC, 2 * GC), GC)
                    nc.gpsimd.tensor_tensor(h_sum, seq_hi[:, cols].bitcast(F32),
                                            seq_lo[:, cols].bitcast(F32), ALU.add).then_inc(hsum_made, 1)
                if b == 1 and exists(g, 2):
                    inverse_deviation(1, g.times(1, -1))
                if b == 2 and exists(g, -2):
                    inverse_deviation(0, g.times(1, 3))
                if b == 3 and exists(g, -2):
                    pool.wait_ge(shift_made[0], seen(g.times(1, 3)))
                    pool.wait_ge(x1t_made, seen(g.times(1, 0)))
                    if g.number >= 1:
                        pool.wait_ge(y_made, seen(g.times(GB, -1)))
                    alone(pool)
                    normalize(0, x1[:, g.ring(3, 2)], resid, None, range(GB - 1))
                if slot_exists(g, b, 4):
                    ring, slot = ring_back(g, b, 4)
                    pool.wait_ge(attended_made, seen(g.times(GB, b - 3)))
                    nc.gpsimd.tensor_tensor(y[:, ring, of(slot)], attended[:, b % 2],
                                            x1[:, ring, of(slot)], ALU.add).then_inc(y_made, 1)
                if b == 2 and exists(g, 2):
                    pool.wait_ge(shift_made[1], seen(g.times(1, -1)))
                    pool.wait_ge(stored[g.ring(3, -2)], seen(stores_before(g)))
                    alone(pool)
                    normalize(1, out_tile[:, g.ring(3, -2)], y[:, g.ring(3, -2)], out_made,
                              LAST_SHARE if g.number >= NG else range(GB))
                if b == 3 and exists(g, -2):
                    if g.number >= 1:
                        pool.wait_ge(y_made, seen(g.times(GB, 0)))
                    alone(pool)
                    normalize(0, x1[:, g.ring(3, 2)], resid, x1_made, range(GB - 1, GB))

            lstm_phase(pool, lstm_step, attention_slot, POOL_SLOTS_AFTER)
            for g in attention_turns(pool):
                for b in range(1 if g.number == 0 else 0, GB):
                    attention_slot(g, b)

        @block.scalar
        def _(act):
            act.dma_start(w1[:], Wg1).then_inc(weights_in, 16)
            act.dma_start(b1_rows[:], bg1.rearrange("(o d) -> o d", o=1).broadcast_to([128, D])).then_inc(weights_in, 16)
            act.dma_start(b_in[:, 0], bih.rearrange("p (g k) -> (p g) k", g=4)).then_inc(weights_in, 16)
            act.dma_start(b_in[:, 1], bhh.rearrange("p (g k) -> (p g) k", g=4)).then_inc(weights_in, 16)
            act.dma_start(wqkv[:], Wqkv).then_inc(weights_in, 16)

            def activate(s, gate):
                act.wait_ge(gate_made[gate], seen(s.forgets if gate == GATE_F else s.done))
                n = (s.p - 1) * 4 + gate
                nc.scalar.activation(gates[:, s.stream, gate, 0:COLS[s.p]], bank[:, GATES_AT + gate, 0:COLS[s.p]],
                                     ACT.Tanh, bias=gate_bias[:, n:n + 1],
                                     scale=1.0 if gate == GATE_G else 0.5).then_inc(gate_active[gate], 1)

            def tanh_of_cell(s):
                act.wait_ge(cell_made, seen(s.done))
                nc.scalar.activation(tanh_cell[:, s.stream, 0:COLS[s.p]], cell[:, s.stream, 0:COLS[s.p]],
                                     ACT.Tanh, scale=0.5).then_inc(tanh_made, 1)

            def activate_gates(s, before=None):
                if before and not s.first:
                    tanh_of_cell(before)
                for n, gate in enumerate(FIRST_STEP if s.first else LATER_STEP):
                    if gate == GATE_O:
                        act.wait_ge(state_made, seen(s.done - 2))
                    activate(s, gate)
                    if before and s.first and n == 1 - s.stream:
                        tanh_of_cell(before)

            def halve_weights(n):
                act.wait_ge(wt_made, n + 1)
                nc.scalar.activation(w_half[:, n], bank[:, WT_BANK[n]], ACT.Copy, scale=0.5).then_inc(wt_half, 1)

            for g in graph_turns(act):
                if exists(g):
                    act.wait_ge(ax_made, seen(g.times(1, 1)))
                    act.wait_ge(h0_made, seen(g.times(1, -1)))
                    nc.scalar.activation(ax_sb[:, g.ring(2)], bank[:, AX], ACT.Copy).then_inc(ax_out, 1)
                if exists(g, 1):
                    act.wait_ge(h0_biased, seen(g.times(1, 0)))
                    act.wait_ge(u_made, seen(g.times(1, -2)))
                    nc.scalar.activation(h0[:, g.ring(2, -1)], h0_pre[:, 0], ACT.Relu).then_inc(h0_out, 1)
                if exists(g, 3):
                    act.wait_ge(h1_made, seen(g.times(1, -2)))
                    act.wait_ge(h1_lo, seen(g.times(1, -4)))
                    nc.scalar.activation(h1[:, g.ring(2, -3)], bank[:, H1], ACT.Relu, scale=2.0).then_inc(h1_out, 1)
                for n in weights_now(g):
                    halve_weights(n)
                if g.number == 2:
                    act.wait_ge(setup_out, 3)
                if exists(g, 4):
                    activate_gates(first_lstm_step(g))
                    tanh_of_cell(first_lstm_step(g))

            def attention_slot(g, b):
                if slot_exists(g, b, 1):
                    m = (b - 1) % 2
                    act.wait_ge(max_made, seen(g.times(GB, b)))
                    act.wait_ge(probt_made, seen(g.times(GB, b - 2)))
                    for h in range(HEADS):
                        last = nc.scalar.activation(by_head(prob[:, m])[:, h], by_head(masked[:, m])[:, h],
                                                    ACT.Exp, bias=neg_max[:, m, h:h + 1])
                    last.then_inc(prob_made, 1)
                if slot_exists(g, b, 2):
                    m = b % 2
                    act.wait_ge(probt_made, seen(g.times(GB, b - 1)))
                    act.wait_ge(weighed_made, seen(g.times(GB, b - 3)))
                    nc.scalar.activation(prob_t[:, m], bank[:, PROB_T], ACT.Copy).then_inc(probt_out, 1)
                if b == 0 and exists(g, -1):
                    act.wait_ge(x1t_made, seen(g.times(1, 2)))
                    act.wait_ge(v_made, seen(g.times(1, 1)))
                    act.wait_ge(x1t_lo_made, seen(g.times(1, 1)))
                    nc.scalar.activation(x1_t, bank[:, TRANSPOSES], ACT.Copy).then_inc(x1t_out, 1)
                if b == 2 and exists(g, -1):
                    nxt = g.ring(3, 1)
                    act.wait_ge(k_made, seen(g.times(1, 2)))
                    if g.number >= 2:
                        act.wait_ge(scores_made, seen(g.times(GB, -4)))
                    act.wait_ge(ones_made, 2 * SKIPS + 1)
                    for h in range(HEADS):
                        rows = of(h, HD)
                        last = nc.scalar.activation(k_exp[rows, nxt, h], bank[rows, K_AND_V], ACT.Copy)
                    last.then_inc(k_spread, 1)
                    act.wait_ge(q_made, seen(g.times(1, 2)))
                    nc.scalar.activation(q_t[:, nxt], bank[:, Q], ACT.Copy, scale=HD ** -0.5).then_inc(q_out, 1)

            def lstm_step(s, pair):
                if s.p < SKIPS or pair.number == 0 or s.first and s.stream == 0:
                    activate_gates(s, step_before(s, pair))
                else:
                    activate_gates(s)
                if s.p == SKIPS and pair.number == 1:
                    tanh_of_cell(s)

            lstm_phase(act, lstm_step, attention_slot)
            for g in attention_turns(act):
                for b in range(GB):
                    attention_slot(g, b)

        @block.vector
        def _(dve):
            def rows_of(p_ap, n):
                return p_ap.rearrange("p (o c) -> p o c", o=1).broadcast_to([128, n, p_ap.shape[1]])

            dve.wait_ge(setup_mm, 1)
            nc.vector.tensor_copy(adj_t[:], bank[:, 4, 0:T]).then_inc(setup_out, 1)
            dve.wait_ge(adj_in, 16)
            nc.vector.tensor_scalar(mask[:], adj_nat[:], 0.0, MASKED, ALU.is_equal, ALU.mult).then_inc(mask_made, 1)
            dve.wait_ge(weights_in, 16 * WEIGHT_LOADS)
            nc.vector.tensor_tensor(b_sum[:], b_in[:, 0], b_in[:, 1], ALU.add).then_inc(bsum_made, 1)
            dve.wait_ge(setup_mm, 2)
            nc.vector.tensor_copy(b0_term[:], bank[:, 5, 0:T]).then_inc(setup_out, 1)
            dve.wait_ge(setup_mm, 3)
            by_gate = bank[:, 6, 0:SKIPS * 4].rearrange("u (p g) -> u p g", g=4)
            to_gate = gate_bias[:].rearrange("u (p g) -> u p g", g=4)
            nc.vector.tensor_scalar(to_gate[:, :, GATE_I:GATE_G], by_gate[:, :, GATE_I:GATE_G], 0.5, None, ALU.mult)
            nc.vector.tensor_copy(to_gate[:, :, GATE_G], by_gate[:, :, GATE_G])
            nc.vector.tensor_scalar(to_gate[:, :, GATE_O], by_gate[:, :, GATE_O], 0.5, None, ALU.mult).then_inc(setup_out, 1)
            nc.vector.tensor_copy(wqk_hi[:], wqkv[:, 0:2 * D]).then_inc(wqk_hi_made, 1)
            dve.wait_ge(mask_made, 1)
            dve.wait_ge(setup_out, 2)

            def cell_of(s):
                stream, c = s.stream, COLS[s.p]
                new = cell[:, stream, 0:c] if s.first else added[:, stream, 0:c]
                if not s.first:
                    dve.wait_ge(gate_active[GATE_F], seen(s.forgets))
                    nc.vector.scalar_tensor_tensor(kept[:, stream, 0:c], gates[:, stream, GATE_F, 0:c], 1.0,
                                                   cell[:, stream, 0:c], ALU.add, ALU.mult)
                dve.wait_ge(gate_active[GATE_I], seen(s.done))
                dve.wait_ge(gate_active[GATE_G], seen(s.done))
                nc.vector.scalar_tensor_tensor(new, gates[:, stream, GATE_I, 0:c], 1.0, gates[:, stream, GATE_G, 0:c],
                                               ALU.add, ALU.mult).then_inc(cell_made if s.first else term_made, 1)
                if not s.first:
                    dve.wait_ge(term_made, seen(s.forgets))
                    nc.vector.scalar_tensor_tensor(cell[:, stream, 0:c], kept[:, stream, 0:c], 0.5,
                                                   added[:, stream, 0:c], ALU.mult, ALU.add).then_inc(cell_made, 1)

            def state_of(s):
                stream, c = s.stream, COLS[s.p]
                dve.wait_ge(gate_active[GATE_O], seen(s.done))
                dve.wait_ge(tanh_made, seen(s.done))
                dve.wait_ge(state_lo_made, seen(s.done - 2))
                nc.vector.scalar_tensor_tensor(state[:, stream, 0:c], gates[:, stream, GATE_O, 0:c], 1.0,
                                               tanh_cell[:, stream, 0:c], ALU.add, ALU.mult).then_inc(state_made, 1)
                dve.wait_ge(state_made, seen(s.done))
                alone(dve)
                into = seq_cols(seq_hi, s) if s.last else shaped(state_hi[:, stream], s.p)
                nc.vector.tensor_copy(into, shaped(state[:, stream], s.p)).then_inc(state_hi_made, 1)

            def lstm_step(s, pair):
                cell_of(s)
                if s.first and s.stream == 0 and step_before(s, pair):
                    state_of(step_before(s, pair))
                if not (s.last and s.stream == 1) or s.p == SKIPS and pair.number == 1:
                    state_of(s)

            def weights_hi(n):
                dve.wait_ge(wt_half, seen(n + 1))
                nc.vector.tensor_copy(lstm_weights(*WT[n])[0], w_half[:, n]).then_inc(wt_hi, 1)

            for g in graph_turns(dve):
                if exists(g, 1):
                    dve.wait_ge(h0_made, seen(g.times(1, 0)))
                    dve.wait_ge(h0_out, seen(g.times(1, -1)))
                    nc.vector.tensor_tensor(by_graph(h0_pre[:, 0]), by_graph(bank[:, H0]), rows_of(b0_term[:], GB),
                                            ALU.add).then_inc(h0_biased, 1)
                if exists(g, 2):
                    dve.wait_ge(u_made, seen(g.times(1, -1)))
                    dve.wait_ge(h1_made, seen(g.times(1, -3)))
                    nc.vector.tensor_tensor(by_graph(u_sb[:, g.ring(2, -2)]), by_graph(bank[:, U]), rows_of(b1_rows[:], GB),
                                            ALU.add).then_inc(u_out, 1)
                if exists(g, 5):
                    state_of(first_lstm_step(g, 5))
                if exists(g, 3):
                    dve.wait_ge(h1_out, seen(g.times(1, -2)))
                    alone(dve)
                    nc.vector.tensor_copy(seq_hi[:, bass.ds(g.times(GC, -3 * GC), GC)],
                                          h1[:, g.ring(2, -3)]).then_inc(h1_hi, 1)
                for n in weights_now(g):
                    weights_hi(n)
                if exists(g, 4):
                    cell_of(first_lstm_step(g))
            state_of(first_lstm_step(Turn(NG + 4), 5))

            def moments_of(norm, src, count, last_group=False):
                for b in range(GB):
                    if last_group:
                        dve.wait_ge(y_made, seen(B - GB + b + 1))
                    last = nc.vector.bn_stats(stats[:, b], src[:, of(b)])
                last.then_inc(bn_made[norm], 1)
                dve.wait_ge(bn_made[norm], seen(count))
                alone(dve)
                for b in range(GB):
                    last = nc.vector.bn_aggr(moments[:, norm, b], stats[:, b])
                last.then_inc(mom_made[norm], 1)

            def shift_of(norm, count):
                dve.wait_ge(rstd_made[norm], seen(count))
                nc.vector.scalar_tensor_tensor(shift[:, norm], moments[:, norm, :, 0], -1.0, rstd[:, norm],
                                               ALU.mult, ALU.mult).then_inc(shift_made[norm], 1)

            def attention_slot(g, b):
                if b == 2 and exists(g, 2):
                    shift_of(1, g.times(1, -1))
                if b == 3 and exists(g, -2):
                    shift_of(0, g.times(1, 3))
                if slot_exists(g, b, 4):
                    m, done = b % 2, g.times(GB, b - 3)
                    dve.wait_ge(weighed_made, seen(done))
                    weighed = bank[:, WEIGHED + m, 0:HEADS * VW].rearrange("p (h w) -> p h w", h=HEADS)
                    nc.vector.reciprocal(rec[:, m], weighed[:, :, HD]).then_inc(rec_made, 1)
                    dve.wait_ge(rec_made, seen(done))
                    dve.wait_ge(y_made, seen(g.times(GB, b - 5)))
                    nc.vector.tensor_tensor(attended[:, m].rearrange("p (h w) -> p h w", h=HEADS),
                                            weighed[:, :, 0:HD],
                                            rec[:, m].rearrange("p (h o) -> p h o", o=1).broadcast_to([128, HEADS, HD]),
                                            ALU.mult).then_inc(attended_made, 1)
                if slot_exists(g, b, 0):
                    m = b % 2
                    dve.wait_ge(scores_made, seen(g.times(GB, b + 1)))
                    dve.wait_ge(prob_made, seen(g.times(GB, b - 1)))
                    nc.vector.tensor_tensor(by_head(masked[:, m]), by_head(bank[:, SCORES + m]),
                                            rows_of(mask[:], HEADS), ALU.add).then_inc(masked_made, 1)
                    dve.wait_ge(masked_made, seen(g.times(GB, b + 1)))
                    nc.vector.tensor_reduce(neg_max[:, m], by_head(masked[:, m]), AX_X, ALU.max,
                                            negate=True).then_inc(max_made, 1)
                if b == 0 and exists(g, 2):
                    if g.number <= NG:
                        dve.wait_ge(y_made, seen(g.times(GB, -GB)))
                    moments_of(1, y[:, g.ring(3, -2)], g.times(1, -1), last_group=g.number == NG + 1)
                if b == 1 and exists(g, -2):
                    dve.wait_ge(ht_made, seen(g.times(1, 3)))
                    dve.wait_ge(res_in, g.times(16, 48))
                    dve.wait_ge(x1_made, seen(g.times(1, 2)))
                    nc.vector.scalar_tensor_tensor(resid, bank[:, TRANSPOSES], 0.5, x_res,
                                                   ALU.mult, ALU.add).then_inc(resid_made, 1)
                    dve.wait_ge(resid_made, seen(g.times(1, 3)))
                    moments_of(0, resid, g.times(1, 3))
                if b == 2 and g.number >= NG:
                    dve.wait_ge(shift_made[1], seen(g.number - 1))
                    dve.wait_ge(stored[g.ring(3, -2)], seen(stores_before(g)))
                    for n in range(LAST_SHARE[0]):
                        last = nc.vector.tensor_scalar(out_tile[:, g.ring(3, -2), of(n)], y[:, g.ring(3, -2), of(n)], rstd[:, 1, n:n + 1],
                                                       shift[:, 1, n:n + 1], ALU.mult, ALU.add)
                    last.then_inc(last_out, 1)
                if b == 0 and exists(g, -1):
                    dve.wait_ge(x1t_out, seen(g.times(1, 2)))
                    dve.wait_ge(q_made, seen(g.times(1, 1)))
                    nc.vector.tensor_copy(x1t_hi[:], x1_t).then_inc(x1t_hi_made, 1)
                if b == 0 and exists(g):
                    dve.wait_ge(v_made, seen(g.times(1, 1)))
                    dve.wait_ge(ones_made, 2 * SKIPS + 1)
                    if g.number >= 1:
                        dve.wait_ge(weighed_made, seen(g.times(GB, -8)))
                    nc.vector.tensor_copy(v_aug[:, g.ring(3), :, :, 0:HD].rearrange("p b h w -> p (b h) w"),
                                          bank[:, K_AND_V].rearrange("p (n w) -> p n w", w=HD)).then_inc(v_out, 1)

            lstm_phase(dve, lstm_step, attention_slot)
            for g in attention_turns(dve):
                for b in range(GB):
                    attention_slot(g, b)

        @block.tensor
        def _(pe):
            pe.wait_ge(consts_made, 2)
            pe.wait_ge(adj_in, 16)
            nc.tensor.transpose(bank[:, 4, 0:T], adj_nat[:], ident[:]).then_inc(setup_mm, 1)

            def per_graph(out_bank, stationary, moving, made):
                for b in range(GB):
                    last = nc.tensor.matmul(bank[:, out_bank, of(b)], stationary[:, of(b)], moving, start=True, stop=True)
                last.then_inc(made, 1)

            def product(dst, hi, lo, x_hi, x_lo, start, stop, x_lo_made=None):
                nc.tensor.matmul(dst, hi, x_hi, start=start, stop=False)
                nc.tensor.matmul(dst, lo, x_hi, start=False, stop=False)
                if x_lo_made:
                    pe.wait_ge(*x_lo_made)
                return nc.tensor.matmul(dst, hi, x_lo, start=False, stop=stop)

            def lstm_step(s, pair=None):
                order = FIRST_STEP if s.first else LATER_STEP
                lo_made = None
                if s.first:
                    if s.p == 1:
                        pe.wait_ge(h1_hi, seen(s.done))
                        lo_made = h1_lo, seen(s.done)
                    elif s.p == 2:
                        pe.wait_ge(state_lo_made, seen(pair.times(4, 2 * s.stream + 2)))
                    elif s.p == 3:
                        pe.wait_ge(state_lo_made, seen(pair.times(4, STEPS_BEFORE[2] + 3 + s.stream)))
                    else:
                        pe.wait_ge(state_lo_made, seen(pair.times(12, STEPS_BEFORE[3] + 6 + 6 * s.stream)))
                if s.first and s.p > 1 and pair.number == 0:
                    pe.wait_ge(wt_lo, seen(2 * s.p - 1))
                for gate in order:
                    pe.wait_ge(gate_active[gate], seen((s.forgets if gate == GATE_F else s.done) - 1))
                    last = product(shaped(bank[:, GATES_AT + gate], s.p), wih_hi[:, s.p - 1, of(gate, D)],
                                   wih_lo[:, s.p - 1, of(gate, D)], seq_cols(seq_hi, s), seq_cols(seq_lo, s),
                                   True, s.first, lo_made if gate == order[0] else None)
                    if s.first:
                        last.then_inc(gate_made[gate], 1)
                if not s.first:
                    pe.wait_ge(state_hi_made, seen(s.done - 2))
                    lo_made = state_lo_made, seen(s.done - 2)
                    for gate in order:
                        product(shaped(bank[:, GATES_AT + gate], s.p), whh_hi[:, s.p - 2, of(gate, D)],
                                whh_lo[:, s.p - 2, of(gate, D)], shaped(state_hi[:, s.stream], s.p),
                                shaped(state_lo[:, s.stream], s.p), False, True,
                                lo_made if gate == order[0] else None).then_inc(gate_made[gate], 1)

            def transpose_weights(n):
                if n == 0:
                    pe.wait_ge(first_lstm_in, 16)
                else:
                    pe.wait_ge(lstm_in, 32)
                if n == 0:
                    pe.wait_ge(setup_out, 1)
                elif WT_BANK[n] in WT_BANK[:n]:
                    pe.wait_ge(wt_half, seen(max(m for m in range(n) if WT_BANK[m] == WT_BANK[n]) + 1))
                elif WT_BANK[n] == AX:
                    pe.wait_ge(ax_out, seen(NG))
                elif WT_BANK[n] == H0:
                    pe.wait_ge(h0_biased, seen(NG))
                else:
                    pe.wait_ge(u_out, seen(NG))
                for gate in range(4):
                    last = nc.tensor.transpose(bank[:, WT_BANK[n], of(gate, D)],
                                               w_nat[:, of(matrix_at(n) + gate, D)], ident[:])
                last.then_inc(wt_made, 1)

            for g in graph_turns(pe):
                if exists(g):
                    if g.number == 0:
                        pe.wait_ge(setup_out, 1)
                    pe.wait_ge(x_in[g.ring(2)], transfers(g))
                    pe.wait_ge(ax_out, seen(g.times(1, 0)))
                    per_graph(AX, x_tile[:, g.ring(2)], adj_t[:], ax_made)
                if g.number == 1:
                    pe.wait_ge(weights_in, 16 * WEIGHT_LOADS)
                    nc.tensor.matmul(bank[:, 5, 0:T], b0_rows[:], adj_t[:], start=True, stop=True).then_inc(setup_mm, 1)
                    pe.wait_ge(bsum_made, 1)
                    nc.tensor.transpose(bank[:, 6, 0:SKIPS * 4], b_sum[:], ident[0:SKIPS * 4, 0:SKIPS * 4]).then_inc(setup_mm, 1)
                if exists(g, 1):
                    pe.wait_ge(ax_out, seen(g.times(1, 0)))
                    pe.wait_ge(h0_biased, seen(g.times(1, -1)))
                    nc.tensor.matmul(bank[:, H0], w0[:], ax_sb[:, g.ring(2, -1)], start=True, stop=True).then_inc(h0_made, 1)
                if exists(g, 2):
                    pe.wait_ge(h0_out, seen(g.times(1, -1)))
                    pe.wait_ge(u_out, seen(g.times(1, -2)))
                    per_graph(U, h0[:, g.ring(2, -2)], w1[:], u_made)
                if exists(g, 3):
                    pe.wait_ge(u_out, seen(g.times(1, -2)))
                    pe.wait_ge(h1_out, seen(g.times(1, -3)))
                    per_graph(H1, u_sb[:, g.ring(2, -3)], adj_t[:], h1_made)
                for n in weights_now(g):
                    transpose_weights(n)
                if exists(g, 4):
                    if g.number == 4:
                        pe.wait_ge(wt_lo, seen(1))
                        pe.wait_ge(setup_out, 3)
                    lstm_step(first_lstm_step(g))

            def attention_slot(g, b):
                if slot_exists(g, b, 0):
                    m, now = b % 2, g.ring(3)
                    if b == 0:
                        pe.wait_ge(k_spread, seen(g.times(1, 1)))
                        pe.wait_ge(q_out, seen(g.times(1, 1)))
                    if g.number == 0 and b == 1:
                        pe.wait_ge(gate_active[GATE_O], seen(ALL_STEPS))
                    pe.wait_ge(masked_made, seen(g.times(GB, b - 1)))
                    nc.tensor.matmul(by_head(bank[:, SCORES + m]), q_t[:, now, of(b)],
                                     k_exp[:, now, :, of(b)], start=True, stop=True).then_inc(scores_made, 1)
                if slot_exists(g, b, 2):
                    m = b % 2
                    pe.wait_ge(prob_made, seen(g.times(GB, b - 1)))
                    pe.wait_ge(probt_out, seen(g.times(GB, b - 2)))
                    for h in range(HEADS):
                        last = nc.tensor.transpose(by_head(bank[:, PROB_T])[:, h], by_head(prob[:, m])[:, h], ident[:])
                    last.then_inc(probt_made, 1)
                if b == 1 and exists(g, -2):
                    pe.wait_ge(hsum_made, seen(g.times(1, 3)))
                    pe.wait_ge(x1t_out, seen(g.times(1, 2)))
                    for n in range(GB):
                        last = nc.tensor.transpose(bank[:, TRANSPOSES, of(n)], h_sum[:, of(n)], ident[:])
                    last.then_inc(ht_made, 1)
                if slot_exists(g, b, 3):
                    ring, slot = ring_back(g, b, 3)
                    m = (b - 3) % 2
                    pe.wait_ge(probt_out, seen(g.times(GB, b - 2)))
                    if slot == 0:
                        pe.wait_ge(v_out, seen(g.times(1, 1)))
                    pe.wait_ge(attended_made, seen(g.times(GB, b - 4)))
                    for h in range(HEADS):
                        nc_last = nc.tensor.matmul(bank[:, WEIGHED + m, of(h, VW)], by_head(prob_t[:, m])[:, h],
                                                   v_aug[:, ring, slot, h], start=True, stop=True)
                    nc_last.then_inc(weighed_made, 1)
                if b == 0 and exists(g, -1):
                    pe.wait_ge(x1_made, seen(g.times(1, 2)))
                    pe.wait_ge(resid_made, seen(g.times(1, 2)))
                    for n in range(GB):
                        last = nc.tensor.transpose(bank[:, TRANSPOSES, of(n)], x1[:, g.ring(3, 1), of(n)], ident[:])
                    last.then_inc(x1t_made, 1)
                if b == 1 and exists(g, -1):
                    pe.wait_ge(x1t_hi_made, seen(g.times(1, 2)))
                    pe.wait_ge(v_out, seen(g.times(1, 1)))
                    if g.number == -1:
                        pe.wait_ge(wqk_lo_made, 1)
                    product(bank[:, K_AND_V], wqk_hi[:, of(1, D)], wqk_lo[:, of(1, D)], x1t_hi[:], x1t_lo[:], True, True,
                            (x1t_lo_made, seen(g.times(1, 2)))).then_inc(k_made, 1)
                    pe.wait_ge(q_out, seen(g.times(1, 1)))
                    product(bank[:, Q], wqk_hi[:, of(0, D)], wqk_lo[:, of(0, D)], x1t_hi[:], x1t_lo[:], True,
                            True).then_inc(q_made, 1)
                if b == 3 and exists(g, -1):
                    pe.wait_ge(k_spread, seen(g.times(1, 2)))
                    per_graph(K_AND_V, x1_t, wqkv[:, of(2, D)], v_made)

            lstm_phase(pe, lstm_step, attention_slot, PE_SLOTS_AFTER)
            for g in attention_turns(pe):
                for b in range(GB):
                    attention_slot(g, b)


_INS = ["x", "adj", "L0_gnn_Wg0", "L0_gnn_bg0", "L0_gnn_Wg1", "L0_gnn_bg1", "L0_gnn_Wih", "L0_gnn_Whh",
        "L0_gnn_bih", "L0_gnn_bhh", "L1_gnn_W"]


def kernel(**inputs):
    import numpy as _np
    import concourse.bacc as _bacc
    from concourse import mybir as _mybir
    from concourse.bass_utils import run_bass_kernel_spmd as _run

    nc = _bacc.Bacc("TRN2", target_bir_lowering=False, num_devices=1)
    arrays, args = {}, []
    for name in _INS:
        a = _np.ascontiguousarray(inputs[name])
        arrays[f"in_{name}"] = a
        args.append(nc.dram_tensor(f"in_{name}", a.shape, _mybir.dt.from_np(a.dtype), kind="ExternalInput").ap())
    out = nc.dram_tensor("out_x", inputs["x"].shape, _mybir.dt.from_np(_np.dtype("float32")), kind="ExternalOutput").ap()
    gnn_lstm_attention(nc, *args, out)
    r = _run(nc, [arrays], core_ids=[0])
    return r.results[0]["out_x"]
```
